# Optimizing a Trainium2 kernel written in Bass

```python
import numpy as np
import jax
import jax.numpy as jnp

def _softmax(x, axis=-1):
    return jax.nn.softmax(x, axis=axis)

def _gelu(x):
    return jax.nn.gelu(x, approximate=True)

def _silu(x):
    return jax.nn.silu(x)

def _sigmoid(x):
    return jax.nn.sigmoid(x)

def _layernorm(x, axis=-1, eps=1e-05):
    m = jnp.mean(x, axis=axis, keepdims=True)
    v = jnp.var(x, axis=axis, keepdims=True)
    return (x - m) / jnp.sqrt(v + eps)

def _scatter_add(tgt, idx, src, axis=0):
    return tgt.at[idx].add(src)

def _segment_sum(src, seg, n):
    return jax.ops.segment_sum(src, seg, n)
kernel_name = 'mk_dlrm_tower_d1_rec_r8_c4f279'

def setup_inputs(seed: int=0):
    np.random.seed(seed)
    _w = jnp.asarray

    def _rec_inputs():
        import jax
        import jax.numpy as jnp
        _tk = jax.random.key(seed)
        dense_ctx = jax.random.normal(jax.random.fold_in(_tk, 190), (1024, 16), jnp.float32)
        ids = jnp.stack([jax.random.randint(jax.random.fold_in(_tk, 200 + f), (1024,), 0, v, jnp.int32) for f, v in enumerate([1000, 12500, 1250, 1000, 125000, 1250, 1000, 1250, 1000, 1250, 12500, 1000, 1250, 12500, 125000, 12500, 12500, 12500, 12500, 1250, 125000, 1250, 1000, 12500, 1000, 1000])], axis=1)
        tbl_0 = 0.05 * jax.random.normal(jax.random.fold_in(_tk, 500 + 0), (1000, 32), jnp.float32)
        tbl_1 = 0.05 * jax.random.normal(jax.random.fold_in(_tk, 500 + 1), (12500, 32), jnp.float32)
        tbl_2 = 0.05 * jax.random.normal(jax.random.fold_in(_tk, 500 + 2), (1250, 32), jnp.float32)
        tbl_3 = 0.05 * jax.random.normal(jax.random.fold_in(_tk, 500 + 3), (1000, 32), jnp.float32)
        tbl_4 = 0.05 * jax.random.normal(jax.random.fold_in(_tk, 500 + 4), (125000, 32), jnp.float32)
        tbl_5 = 0.05 * jax.random.normal(jax.random.fold_in(_tk, 500 + 5), (1250, 32), jnp.float32)
        tbl_6 = 0.05 * jax.random.normal(jax.random.fold_in(_tk, 500 + 6), (1000, 32), jnp.float32)
        tbl_7 = 0.05 * jax.random.normal(jax.random.fold_in(_tk, 500 + 7), (1250, 32), jnp.float32)
        tbl_8 = 0.05 * jax.random.normal(jax.random.fold_in(_tk, 500 + 8), (1000, 32), jnp.float32)
        tbl_9 = 0.05 * jax.random.normal(jax.random.fold_in(_tk, 500 + 9), (1250, 32), jnp.float32)
        tbl_10 = 0.05 * jax.random.normal(jax.random.fold_in(_tk, 500 + 10), (12500, 32), jnp.float32)
        tbl_11 = 0.05 * jax.random.normal(jax.random.fold_in(_tk, 500 + 11), (1000, 32), jnp.float32)
        tbl_12 = 0.05 * jax.random.normal(jax.random.fold_in(_tk, 500 + 12), (1250, 32), jnp.float32)
        tbl_13 = 0.05 * jax.random.normal(jax.random.fold_in(_tk, 500 + 13), (12500, 32), jnp.float32)
        tbl_14 = 0.05 * jax.random.normal(jax.random.fold_in(_tk, 500 + 14), (125000, 32), jnp.float32)
        tbl_15 = 0.05 * jax.random.normal(jax.random.fold_in(_tk, 500 + 15), (12500, 32), jnp.float32)
        tbl_16 = 0.05 * jax.random.normal(jax.random.fold_in(_tk, 500 + 16), (12500, 32), jnp.float32)
        tbl_17 = 0.05 * jax.random.normal(jax.random.fold_in(_tk, 500 + 17), (12500, 32), jnp.float32)
        tbl_18 = 0.05 * jax.random.normal(jax.random.fold_in(_tk, 500 + 18), (12500, 32), jnp.float32)
        tbl_19 = 0.05 * jax.random.normal(jax.random.fold_in(_tk, 500 + 19), (1250, 32), jnp.float32)
        tbl_20 = 0.05 * jax.random.normal(jax.random.fold_in(_tk, 500 + 20), (125000, 32), jnp.float32)
        tbl_21 = 0.05 * jax.random.normal(jax.random.fold_in(_tk, 500 + 21), (1250, 32), jnp.float32)
        tbl_22 = 0.05 * jax.random.normal(jax.random.fold_in(_tk, 500 + 22), (1000, 32), jnp.float32)
        tbl_23 = 0.05 * jax.random.normal(jax.random.fold_in(_tk, 500 + 23), (12500, 32), jnp.float32)
        tbl_24 = 0.05 * jax.random.normal(jax.random.fold_in(_tk, 500 + 24), (1000, 32), jnp.float32)
        tbl_25 = 0.05 * jax.random.normal(jax.random.fold_in(_tk, 500 + 25), (1000, 32), jnp.float32)
        _rk = jax.random.fold_in(_tk, 7)
        W_top1 = 0.0606339 * jax.random.normal(jax.random.fold_in(_tk, 801), (272, 512), jnp.float32)
        W_top2 = 0.0441942 * jax.random.normal(jax.random.fold_in(_tk, 802), (512, 256), jnp.float32)
        W_top3 = 0.0625 * jax.random.normal(jax.random.fold_in(_tk, 803), (256, 1), jnp.float32)
        b_top1 = jnp.zeros((512,), jnp.float32)
        b_top2 = jnp.zeros((256,), jnp.float32)
        return (dense_ctx, ids, tbl_0, tbl_1, tbl_2, tbl_3, tbl_4, tbl_5, tbl_6, tbl_7, tbl_8, tbl_9, tbl_10, tbl_11, tbl_12, tbl_13, tbl_14, tbl_15, tbl_16, tbl_17, tbl_18, tbl_19, tbl_20, tbl_21, tbl_22, tbl_23, tbl_24, tbl_25, W_top1, b_top1, W_top2, b_top2, W_top3)
    dense_ctx, ids, tbl_0, tbl_1, tbl_2, tbl_3, tbl_4, tbl_5, tbl_6, tbl_7, tbl_8, tbl_9, tbl_10, tbl_11, tbl_12, tbl_13, tbl_14, tbl_15, tbl_16, tbl_17, tbl_18, tbl_19, tbl_20, tbl_21, tbl_22, tbl_23, tbl_24, tbl_25, W_top1, b_top1, W_top2, b_top2, W_top3 = _rec_inputs()

    def _L0_rec_setup():
        import jax, jax.numpy as jnp
        import numpy as np
        M_FIELDS = 26
        H1 = 128
        H2 = 128
        BATCH = 256
        EMB_K = 32

        def _cin_layer(x_prev, x0, W, b):
            return jnp.einsum('bik,bjk,hij->bhk', x_prev, x0, W) + b[None, :, None]
        key = jax.random.key(seed)
        k0, k1, k2, k3, k4 = jax.random.split(key, 5)
        inputs = jax.random.normal(k0, (BATCH, M_FIELDS, EMB_K), dtype=jnp.float32)
        W1 = jax.random.normal(k1, (H1, M_FIELDS, M_FIELDS), dtype=jnp.float32) * 0.05
        b1 = jax.random.normal(k2, (H1,), dtype=jnp.float32) * 0.05
        W2 = jax.random.normal(k3, (H2, H1, M_FIELDS), dtype=jnp.float32) * 0.05
        b2 = jax.random.normal(k4, (H2,), dtype=jnp.float32) * 0.05
        return {'inputs': inputs, 'W1': W1, 'b1': b1, 'W2': W2, 'b2': b2}
    _L0_rec_all = _L0_rec_setup()
    _L0_rec_in = {k: v for k, v in _L0_rec_all.items() if k in ('W1', 'b1', 'W2', 'b2')}
    del _L0_rec_all
    return {'dense_ctx': dense_ctx, 'ids': ids, 'tbl_0': tbl_0, 'tbl_1': tbl_1, 'tbl_2': tbl_2, 'tbl_3': tbl_3, 'tbl_4': tbl_4, 'tbl_5': tbl_5, 'tbl_6': tbl_6, 'tbl_7': tbl_7, 'tbl_8': tbl_8, 'tbl_9': tbl_9, 'tbl_10': tbl_10, 'tbl_11': tbl_11, 'tbl_12': tbl_12, 'tbl_13': tbl_13, 'tbl_14': tbl_14, 'tbl_15': tbl_15, 'tbl_16': tbl_16, 'tbl_17': tbl_17, 'tbl_18': tbl_18, 'tbl_19': tbl_19, 'tbl_20': tbl_20, 'tbl_21': tbl_21, 'tbl_22': tbl_22, 'tbl_23': tbl_23, 'tbl_24': tbl_24, 'tbl_25': tbl_25, 'W_top1': W_top1, 'b_top1': b_top1, 'W_top2': W_top2, 'b_top2': b_top2, 'W_top3': W_top3, 'L0_rec_W1': _L0_rec_in['W1'], 'L0_rec_b1': _L0_rec_in['b1'], 'L0_rec_W2': _L0_rec_in['W2'], 'L0_rec_b2': _L0_rec_in['b2']}

def reference(dense_ctx, ids, tbl_0, tbl_1, tbl_2, tbl_3, tbl_4, tbl_5, tbl_6, tbl_7, tbl_8, tbl_9, tbl_10, tbl_11, tbl_12, tbl_13, tbl_14, tbl_15, tbl_16, tbl_17, tbl_18, tbl_19, tbl_20, tbl_21, tbl_22, tbl_23, tbl_24, tbl_25, W_top1, b_top1, W_top2, b_top2, W_top3, L0_rec_W1, L0_rec_b1, L0_rec_W2, L0_rec_b2):
    import jax
    import jax.numpy as jnp

    def _L0_rec_ref(inputs, W1, b1, W2, b2):
        import jax, jax.numpy as jnp
        import numpy as np
        M_FIELDS = 26
        H1 = 128
        H2 = 128
        BATCH = 256
        EMB_K = 32

        def _cin_layer(x_prev, x0, W, b):
            return jnp.einsum('bik,bjk,hij->bhk', x_prev, x0, W) + b[None, :, None]
        x1 = _cin_layer(inputs, inputs, W1, b1)
        x2 = _cin_layer(x1, inputs, W2, b2)
        res = jnp.concatenate([x1, x2], axis=1)
        return jnp.sum(res, axis=-1)
    e = jnp.stack([tbl_0[ids[:, 0]], tbl_1[ids[:, 1]], tbl_2[ids[:, 2]], tbl_3[ids[:, 3]], tbl_4[ids[:, 4]], tbl_5[ids[:, 5]], tbl_6[ids[:, 6]], tbl_7[ids[:, 7]], tbl_8[ids[:, 8]], tbl_9[ids[:, 9]], tbl_10[ids[:, 10]], tbl_11[ids[:, 11]], tbl_12[ids[:, 12]], tbl_13[ids[:, 13]], tbl_14[ids[:, 14]], tbl_15[ids[:, 15]], tbl_16[ids[:, 16]], tbl_17[ids[:, 17]], tbl_18[ids[:, 18]], tbl_19[ids[:, 19]], tbl_20[ids[:, 20]], tbl_21[ids[:, 21]], tbl_22[ids[:, 22]], tbl_23[ids[:, 23]], tbl_24[ids[:, 24]], tbl_25[ids[:, 25]]], axis=1)
    z = _L0_rec_ref(e, L0_rec_W1, L0_rec_b1, L0_rec_W2, L0_rec_b2)
    z = z.reshape(z.shape[0], -1)
    h = jnp.concatenate([z, dense_ctx], axis=1)
    h = jnp.maximum(h @ W_top1 + b_top1, 0.0)
    h = jnp.maximum(h @ W_top2 + b_top2, 0.0)
    y = h @ W_top3
    return y

_drawn_inputs = setup_inputs


def setup_inputs(seed=0):
    import zlib

    import numpy as np

    out = dict(_drawn_inputs(seed))
    spreads = {'b_top1': (0.0, 2.0), 'b_top2': (0.0, 0.8)}
    factors = {'tbl_0': 8.0,
     'tbl_1': 8.0,
     'tbl_2': 8.0,
     'tbl_3': 8.0,
     'tbl_4': 8.0,
     'tbl_5': 8.0,
     'tbl_6': 8.0,
     'tbl_7': 8.0,
     'tbl_8': 8.0,
     'tbl_9': 8.0,
     'tbl_10': 8.0,
     'tbl_11': 8.0,
     'tbl_12': 8.0,
     'tbl_13': 8.0,
     'tbl_14': 8.0,
     'tbl_15': 8.0,
     'tbl_16': 8.0,
     'tbl_17': 8.0,
     'tbl_18': 8.0,
     'tbl_19': 8.0,
     'tbl_20': 8.0,
     'tbl_21': 7.892,
     'tbl_22': 8.0,
     'tbl_23': 8.0,
     'tbl_24': 8.0,
     'tbl_25': 8.0,
     'L0_rec_W1': 7.81,
     'L0_rec_W2': 4.086,
     'dense_ctx': 5.608}
    for name, (base, spread) in spreads.items():
        noise = np.random.default_rng([zlib.crc32(name.encode()), seed]).standard_normal(out[name].shape)
        drawn = base * np.exp(spread * noise) if base else spread * noise
        out[name] = jnp.asarray(drawn.astype(out[name].dtype))
    for name, factor in factors.items():
        out[name] = (out[name] * factor).astype(out[name].dtype)
    return out
```

```python
from contextlib import ExitStack

import concourse.bass as bass
from concourse import mybir

F32 = mybir.dt.float32
I32 = mybir.dt.int32
U32 = mybir.dt.uint32
ALU = mybir.AluOpType
ACT = mybir.ActivationFunctionType
AX_X = mybir.AxisListType.X

B = 1024
F = 26
K = 32
H = 128
DC = 16
N1 = 512
N2 = 256
TILE = 128
Q = TILE // K
NB = K
HALF = NB // 2
QUAD = 4
BLOCK = 2 * TILE
NBLK = B // BLOCK
QUADS_HALF = HALF // QUAD
QUADS_TILE = NB // QUAD
QUADS_BLK = 2 * QUADS_TILE

GROUPS = [(11, 26), (5, 11), (0, 5)]
LS = [hi for _, hi in GROUPS]
PN = [sum(F - b for b in range(lo, hi)) for lo, hi in GROUPS]
PW = max(PN)
SLOT0 = [sum(n + 1 for n in LS[:g]) for g in range(3)]
SLOTS = sum(n + 1 for n in LS)
SUBSLOT = [0, 0, LS[1] + 1]
SUBS = LS[1] + 1 + LS[2] + 1
GROUP_OF = [next(g for g, (lo, hi) in enumerate(GROUPS) if lo <= b < hi) for b in range(F)]
COL = [sum(F - x for x in range(GROUPS[GROUP_OF[b]][0], b)) for b in range(F)]
L1 = F + 1

CUT = 13
MA = CUT * F
MB = MA + (F - CUT) * (F - CUT)
MW = MB + 1


def at(i, j):
    return F * i + j if i < CUT else MA + (F - CUT) * (i - CUT) + (j - CUT)


def tower_kernel(nc, dense, ids, tables, wt1, bt1, wt2, bt2, wt3, cw1, cb1, cw2, cb2, out):
    with ExitStack() as ctx:
        def sb(name, shape, dt=F32):
            return ctx.enter_context(nc.sbuf_tensor(name, shape, dt))

        def bank(name):
            return ctx.enter_context(nc.psum_tensor(name, [128, 512], F32))

        def sem(name):
            return ctx.enter_context(nc.semaphore(name))

        P_N = HALF * 3 * PW
        CS0_N = L1 * BLOCK
        CS12_N = SUBS * BLOCK
        M_N = F * MW
        TC_N = SLOTS * PW
        W2T_N = F * H
        arena = sb("arena", [128, max(2 * P_N + CS0_N + CS12_N, M_N + TC_N + W2T_N)])
        P = arena[:, 0:2 * P_N].rearrange("p (r i c) -> p r i c", r=2, i=HALF)
        CS0 = arena[:, 2 * P_N:2 * P_N + CS0_N].rearrange("p (l b) -> p l b", b=BLOCK)
        CS12 = arena[:, 2 * P_N + CS0_N:2 * P_N + CS0_N + CS12_N].rearrange("p (l b) -> p l b", b=BLOCK)
        M = arena[:, 0:M_N].rearrange("p (l c) -> p l c", c=MW)
        Tc = arena[:, M_N:M_N + TC_N].rearrange("p (s c) -> p s c", c=PW)
        W2nat = arena[:, M_N:M_N + H * F].rearrange("p (i l) -> p i l", l=F)
        W2T = arena[:, M_N + TC_N:M_N + TC_N + W2T_N].rearrange("p (l h) -> p l h", h=H)

        E = sb("E", [128, 2, F, K])
        XT = sb("XT", [128, 2, F, NB])
        BD = sb("BD", [128, 2, NB, Q, L1])
        S = sb("S", [128, 2, F])
        TW = sb("TW", [PW, SLOTS, H])
        VT = sb("VT", [F, H])
        W1raw = sb("W1raw", [128, F, F])
        W1s = sb("W1s", [128, MW])
        ident = sb("ident", [128, 128])
        ids_all = sb("ids_all", [128, B // TILE, F], I32)
        ids_now = sb("ids_now", [128, 2, F], I32)
        rows = sb("rows", [10, 128])
        cols = sb("cols", [128, 10])
        kb = sb("kb", [128, 2])
        densN = sb("densN", [128, B // TILE, DC])
        densT = sb("densT", [DC, B])
        A1 = sb("A1", [128, 2, N1])
        A1d = sb("A1d", [DC, N1])
        A2 = sb("A2", [128, N1 // 128, N2])
        ST = sb("ST", [F, BLOCK])
        ZT = sb("ZT", [128, 2, BLOCK])
        H1T = sb("H1T", [128, N1 // 128, BLOCK])
        H2T = sb("H2T", [128, N2 // 128, BLOCK])
        Y = sb("Y", [1, B])

        pC0 = [bank("pC0a"), bank("pC0b")]
        pC12 = [bank("pC12a"), bank("pC12b")]
        pZ = bank("pZ")
        pH = [bank("pHa"), bank("pHb")]
        pG = bank("pG")
        C0v = [p[0:PN[0], 0:QUAD * Q * L1].rearrange("p (i q l) -> p i q l", q=Q, l=L1) for p in pC0]
        C12v = [p[0:PW, 0:QUAD * Q * SUBS].rearrange("p (i q l) -> p i q l", q=Q, l=SUBS) for p in pC12]

        ids_loaded = sem("ids_loaded")
        w1_loaded = sem("w1_loaded")
        w2_loaded = sem("w2_loaded")
        rows_loaded = sem("rows_loaded")
        dense_loaded = sem("dense_loaded")
        top_loaded = sem("top_loaded")
        ident_zero = sem("ident_zero")
        ident_ready = sem("ident_ready")
        ids_staged = sem("ids_staged")
        gathers_begun = sem("gathers_begun")
        gathered = [sem("gathered_even"), sem("gathered_odd")]
        zeroed = sem("zeroed")
        w1_step = sem("w1_step")
        pre_psum = sem("pre_psum")
        pre_out = sem("pre_out")
        folded = sem("folded")
        slot0_copied = sem("slot0_copied")
        e_used = sem("e_used")
        xt_ready = sem("xt_ready")
        bd_ready = sem("bd_ready")
        s_ready = sem("s_ready")
        p_ready = sem("p_ready")
        c0_done = sem("c0_done")
        c12_done = sem("c12_done")
        c0_out = sem("c0_out")
        c12_out = sem("c12_out")
        st_psum = sem("st_psum")
        st_out = sem("st_out")
        z_psum = sem("z_psum")
        z_out = sem("z_out")
        h1_psum = sem("h1_psum")
        h1_out = sem("h1_out")
        h2_psum = sem("h2_psum")
        h2_out = sem("h2_out")
        y_psum = sem("y_psum")
        y_out = sem("y_out")
        stored = sem("stored")

        PB = [pC0[0], pC0[1], pC12[0], pC12[1], pZ, pH[0], pH[1], pG]
        four = lambda n: [list(range(x, min(x + 4, n))) for x in range(0, n, 4)]
        prep = [("cols", [0])]
        prep += [("w2t", g) for g in four(F)]
        prep += [("m", [l]) for l in range(F)]
        prep += [("dense", g) for g in four(B // TILE)]
        N_M = sum(kind in ("cols", "w2t", "m") for kind, _ in prep)
        prep += [("tw", g) for g in four(SLOTS)] + [("vt", [0])]
        N_PREP = len(prep)
        W2T_OUT = 1 + len(four(F))

        def group_of_slot(s):
            return 0 if s < SLOT0[1] else 1 if s < SLOT0[2] else 2

        block = ctx.enter_context(nc.Block())

        @block.sync
        def _(sp):
            sp.dma_start(ids_all[:], ids.rearrange("(t p) f -> p t f", p=TILE)).then_inc(ids_loaded, 16)
            sp.dma_start(W2nat, cw2).then_inc(w2_loaded, 16)
            sp.dma_start(W1raw[:], cw1).then_inc(w1_loaded, 16)
            sp.dma_start(rows[0:4, :], bt1.rearrange("(a b) -> a b", b=128)).then_inc(rows_loaded, 16)
            sp.dma_start(rows[4:6, :], bt2.rearrange("(a b) -> a b", b=128)).then_inc(rows_loaded, 16)
            sp.dma_start(rows[6:8, :], wt3.rearrange("(a b) o -> a (b o)", b=128)).then_inc(rows_loaded, 16)
            sp.dma_start(rows[8:9, :], cb1.rearrange("(a b) -> a b", a=1)).then_inc(rows_loaded, 16)
            sp.dma_start(rows[9:10, :], cb2.rearrange("(a b) -> a b", a=1)).then_inc(rows_loaded, 16)
            sp.dma_start(densN[:], dense.rearrange("(t p) f -> p t f", p=TILE)).then_inc(dense_loaded, 16)
            sp.dma_start(A1[:], wt1[0:2 * H, :].rearrange("(c p) n -> p c n", p=128)).then_inc(top_loaded, 16)
            sp.dma_start(A1d[:], wt1[2 * H:2 * H + DC, :]).then_inc(top_loaded, 16)
            sp.dma_start(A2[:], wt2.rearrange("(c p) n -> p c n", p=128)).then_inc(top_loaded, 16)
            sp.wait_ge(y_out, NBLK)
            sp.dma_start(out.rearrange("b o -> o b"), Y[:]).then_inc(stored, 16)
            sp.wait_ge(stored, 16)

        @block.gpsimd
        def _(pool):
            nc.gpsimd.memset(ident[:], 0.0).then_inc(ident_zero, 1)
            pool.wait_ge(ident_zero, 1)
            nc.gpsimd.affine_select(out=ident[:], in_=ident[:], compare_op=ALU.not_equal, fill=1.0, base=0,
                                    pattern=[[-1, 128]], channel_multiplier=1).then_inc(ident_ready, 1)

            pool.wait_ge(ids_loaded, 16)

            def tile(n, s, first):
                if not first:
                    pool.wait_ge(gathered[s], 16 * F * n)
                nc.gpsimd.tensor_copy(ids_now[:, s, :],
                                      ids_all[:, bass.ds(2 * n + s, 1), :].rearrange("p o f -> p (o f)")
                                      ).then_inc(ids_staged, 1)
                pool.wait_ge(ids_staged, 2 * n + s + 1)
                if not first:
                    pool.wait_ge(e_used, 2 * n + s - 1)
                pool.sem_inc(gathers_begun, 1)
                for f in range(F):
                    nc.gpsimd.indirect_dma_start(
                        out=E[:, s, f, :], out_offset=None, in_=tables[f],
                        in_offset=bass.IndirectOffsetOnAxis(ap=ids_now[:, s, f:f + 1].bitcast(U32), axis=0),
                    ).then_inc(gathered[s], 16)

            for s in range(2):
                tile(0, s, True)
            with pool.Fori(1, NBLK) as n:
                for s in range(2):
                    tile(n, s, False)

        @block.vector
        def _(dve):
            nc.vector.memset(BD[:], 0.0).then_inc(zeroed, 1)
            dve.wait_ge(zeroed, 1)
            for s in range(2):
                for q in range(Q):
                    nc.vector.memset(BD[K * q:K * q + K, s, :, q, 0], 1.0).then_inc(zeroed, 1)
            dve.wait_ge(w1_loaded, 16)
            w1t = W1raw[:].rearrange("p i j -> p j i")
            nc.vector.tensor_tensor(W1s[:, 0:MA].rearrange("p (i j) -> p i j", j=F), W1raw[:, 0:CUT, :],
                                    w1t[:, 0:CUT, :], ALU.add).then_inc(w1_step, 1)
            nc.vector.tensor_tensor(W1s[:, MA:MB].rearrange("p (i j) -> p i j", j=F - CUT), W1raw[:, CUT:F, CUT:F],
                                    w1t[:, CUT:F, CUT:F], ALU.add).then_inc(w1_step, 1)
            dve.wait_ge(w1_step, 2)
            flat = W1raw[:].rearrange("p i j -> p (i j)")
            nc.vector.tensor_copy(W1s[:, 0:MA:F + 1], flat[:, 0:MA:F + 1]).then_inc(w1_step, 1)
            nc.vector.tensor_copy(W1s[:, MA:MB:F - CUT + 1], flat[:, at(0, 0) + (F + 1) * CUT::F + 1]).then_inc(w1_step, 1)
            dve.wait_ge(pre_out, 1)
            nc.vector.tensor_copy(W1s[:, MB:MW], cols[:, 8:9]).then_inc(w1_step, 1)
            nc.vector.tensor_scalar(kb[:], cols[:, 8:10], float(K), None, ALU.mult).then_inc(w1_step, 1)
            dve.wait_ge(pre_out, W2T_OUT)
            nc.vector.memset(Tc, 0.0).then_inc(zeroed, 1)
            dve.wait_ge(zeroed, 2 + 2 * Q)
            dve.wait_ge(w1_step, 6)
            for b in range(F):
                g = GROUP_OF[b]
                nc.vector.tensor_copy(Tc[:, SLOT0[g], COL[b]:COL[b] + F - b], W1s[:, at(b, b):at(b, b) + F - b])
            dve.wait_ge(pre_out, N_M)

            def parts(n):
                return [(x, y) for x, y in ((0, min(n, CUT)), (CUT, n)) if x < y]

            def m_rows(l, a0, a1, c0, c1):
                step = F if a0 < CUT else F - CUT
                return bass.AP(tensor=M.tensor, offset=M.offset + l * MW + at(a0, c0),
                               ap=[list(M.ap[0]), [step, a1 - a0], [1, c1 - c0]])

            def m_cols(c0, c1, a0, a1, b):
                step = F if a0 < CUT else F - CUT
                return bass.AP(tensor=M.tensor, offset=M.offset + c0 * MW + at(a0, b),
                               ap=[list(M.ap[0]), [step, a1 - a0], [MW, c1 - c0]])

            for b in range(F):
                s0, x = SLOT0[GROUP_OF[b]] + 1, COL[b]
                for a0, a1 in parts(b):
                    nc.vector.tensor_tensor(Tc[:, s0 + a0:s0 + a1, x:x + F - b], M[:, a0:a1, at(b, b):at(b, b) + F - b],
                                            m_rows(b, a0, a1, b, F), ALU.add)
                last = nc.vector.tensor_copy(Tc[:, s0 + b, x:x + F - b], M[:, b, at(b, b):at(b, b) + F - b])
            last.then_inc(folded, 1)
            dve.wait_ge(folded, 1)
            for b in range(F - 1):
                s0, x = SLOT0[GROUP_OF[b]] + 1, COL[b]
                for a0, a1 in parts(b + 1):
                    t = Tc[:, s0 + a0:s0 + a1, x + 1:x + F - b]
                    last = nc.vector.tensor_tensor(t, t, m_cols(b + 1, F, a0, a1, b), ALU.add)
            last.then_inc(folded, 1)
            dve.wait_ge(folded, 2)
            dve.wait_ge(pre_psum, N_PREP)
            nc.vector.memset(P[:, :, :, PW + PN[1]:2 * PW], 0.0).then_inc(zeroed, 1)

            def tile(n, s, first):
                dve.wait_ge(gathered[s], 16 * F * (n + 1))
                nc.vector.transpose(XT[:, s].rearrange("p f i -> p (f i)"),
                                    E[:, s].rearrange("p f k -> p (f k)")).then_inc(xt_ready, 1)
                if not first:
                    dve.wait_ge(st_psum, n)
                nc.vector.tensor_reduce(S[:, s, :], E[:, s], AX_X, ALU.add).then_inc(e_used, 1)
                dve.wait_ge(xt_ready, 2 * n + s + 1)
                if not first:
                    dve.wait_ge(c12_done, QUADS_TILE * (2 * n + s - 1))
                for q in range(Q):
                    r = slice(K * q, K * q + K)
                    last = nc.vector.tensor_copy(BD[r, s, :, q, 1:L1], XT[r, s].rearrange("p f i -> p i f"))
                last.then_inc(bd_ready, 1)
                for half in range(2):
                    if not (first and s == 0):
                        dve.wait_ge(c12_done, QUADS_HALF * (4 * n + 2 * s + half - 1))
                    i0 = HALF * half
                    for b in range(F):
                        x = PW * GROUP_OF[b] + COL[b]
                        last = nc.vector.tensor_tensor(
                            P[:, half, :, x:x + F - b],
                            XT[:, s, b:F, i0:i0 + HALF].rearrange("p c i -> p i c"),
                            XT[:, s, b, i0:i0 + HALF].unsqueeze(2).broadcast_to([128, HALF, F - b]), ALU.mult)
                    last.then_inc(p_ready, 1)

            for s in range(2):
                tile(0, s, True)
            with dve.Fori(1, NBLK) as n:
                for s in range(2):
                    tile(n, s, False)

        @block.scalar
        def _(act):
            for i, (kind, g) in enumerate(prep):
                src = PB[i % len(PB)]
                if kind == "cols":
                    dst, view = cols[:], src[:, 0:10]
                elif kind == "w2t":
                    dst, view = W2T[:, g[0]:g[-1] + 1, :], src[:, 0:len(g) * H].rearrange("p (l h) -> p l h", h=H)
                elif kind == "m":
                    dst, view = M[:, g[0], :], src[:, 0:MW]
                elif kind == "dense":
                    dst, view = densT[:, g[0] * TILE:(g[-1] + 1) * TILE], src[0:DC, 0:len(g) * TILE]
                elif kind == "tw":
                    dst, view = TW[:, g[0]:g[-1] + 1, :], src[0:PW, 0:len(g) * H].rearrange("p (s h) -> p s h", h=H)
                else:
                    dst, view = VT[:], src[0:F, 0:H]
                act.wait_ge(pre_psum, i + 1)
                nc.scalar.copy(dst, view).then_inc(pre_out, 1)

            def quad(n, s, j):
                v = QUADS_BLK * n + QUADS_TILE * s + j
                i0 = TILE * s + QUAD * j
                act.wait_ge(c0_done, v + 1)
                for i in range(QUAD):
                    last = nc.scalar.copy(CS0[0:PN[0], :, i0 + i:i0 + i + TILE - K + 1:K].rearrange("p l q -> p q l"),
                                          C0v[j % 2][:, i])
                last.then_inc(c0_out, 1)
                act.wait_ge(c12_done, v + 1)
                for i in range(QUAD):
                    last = nc.scalar.copy(CS12[0:PW, :, i0 + i:i0 + i + TILE - K + 1:K].rearrange("p l q -> p q l"),
                                          C12v[j % 2][:, i])
                last.then_inc(c12_out, 1)

            def mlp1(n):
                for c in range(2):
                    act.wait_ge(h1_psum, 2 * n + c + 1)
                    for d in range(2):
                        last = nc.scalar.activation(H1T[:, 2 * c + d, :], pH[c][:, BLOCK * d:BLOCK * (d + 1)], ACT.Relu,
                                                    bias=cols[:, 2 * c + d:2 * c + d + 1])
                    last.then_inc(h1_out, 1)

            def mlp2(n):
                act.wait_ge(h2_psum, n + 1)
                for d in range(2):
                    last = nc.scalar.activation(H2T[:, d, :], pG[:, BLOCK * d:BLOCK * (d + 1)], ACT.Relu,
                                                bias=cols[:, 4 + d:5 + d])
                last.then_inc(h2_out, 1)

            def mlp3(n):
                act.wait_ge(y_psum, n + 1)
                nc.scalar.copy(Y[:, bass.ds(n * BLOCK, BLOCK)], pH[0][0:1, 0:BLOCK]).then_inc(y_out, 1)

            def row_sums(n):
                act.wait_ge(st_psum, n + 1)
                nc.scalar.copy(ST[:], pG[0:F, 0:BLOCK]).then_inc(st_out, 1)

            def z_rows(n):
                act.wait_ge(z_psum, n + 1)
                for d in range(2):
                    last = nc.scalar.activation(ZT[:, d, :], pZ[:, BLOCK * d:BLOCK * (d + 1)], ACT.Identity,
                                                bias=kb[:, d:d + 1])
                last.then_inc(z_out, 1)

            def blk(n, first):
                for j in range(QUADS_TILE):
                    quad(n, 0, j)
                if not first:
                    mlp1(n - 1)
                for j in range(QUADS_TILE):
                    quad(n, 1, j)
                    if j == QUADS_HALF:
                        row_sums(n)
                if not first:
                    mlp2(n - 1)
                z_rows(n)
                if not first:
                    mlp3(n - 1)

            act.wait_ge(w1_step, 6)
            blk(0, True)
            with act.Fori(1, NBLK) as n:
                blk(n, False)
            mlp1(NBLK - 1)
            mlp2(NBLK - 1)
            mlp3(NBLK - 1)

        @block.tensor
        def _(pe):
            pe.wait_ge(ident_ready, 1)
            for i, (kind, g) in enumerate(prep):
                dst = PB[i % len(PB)]
                if i >= len(PB):
                    pe.wait_ge(pre_out, i - len(PB) + 1)
                if kind == "cols":
                    pe.wait_ge(rows_loaded, 16 * 5)
                    last = nc.tensor.transpose(dst[:, 0:10], rows[:], ident[0:10, 0:10])
                elif kind == "w2t":
                    pe.wait_ge(w2_loaded, 16)
                    for x, l in enumerate(g):
                        last = nc.tensor.transpose(dst[:, x * H:(x + 1) * H], W2nat[:, :, l], ident[:])
                elif kind == "m":
                    if g[0] == 0:
                        pe.wait_ge(w1_step, 5)
                        pe.wait_ge(pre_out, W2T_OUT)
                    last = nc.tensor.matmul(dst[:, 0:MW], W2T[:, g[0], :], W1s[:], start=True, stop=True)
                elif kind == "dense":
                    pe.wait_ge(dense_loaded, 16)
                    for x, t in enumerate(g):
                        last = nc.tensor.transpose(dst[0:DC, x * TILE:(x + 1) * TILE], densN[:, t, :], ident[:])
                elif kind == "tw":
                    pe.wait_ge(folded, 2)
                    for x, s in enumerate(g):
                        last = nc.tensor.transpose(dst[0:PW, x * H:(x + 1) * H], Tc[:, s, :], ident[:])
                else:
                    last = nc.tensor.transpose(dst[0:F, 0:H], M[:, :, MB], ident[:])
                last.then_inc(pre_psum, 1)
            pe.wait_ge(pre_out, N_PREP)

            def tile(n, s, first):
                pe.wait_ge(bd_ready, 2 * n + s + 1)
                for j in range(QUADS_TILE):
                    half = j // QUADS_HALF
                    v = QUADS_BLK * n + QUADS_TILE * s + j
                    if s == 1 and j == QUADS_HALF:
                        row_sums(n)
                    if j % QUADS_HALF == 0:
                        pe.wait_ge(p_ready, 4 * n + 2 * s + half + 1)
                    for g in range(3):
                        if g < 2 and not (first and s == 0 and j < 2):
                            pe.wait_ge([c0_out, c12_out][g], v - 1)
                        for i in range(QUAD):
                            step = QUAD * j + i
                            view = C0v[j % 2][:, i] if g == 0 else \
                                C12v[j % 2][:, i, :, SUBSLOT[g]:SUBSLOT[g] + LS[g] + 1]
                            last = nc.tensor.matmul(view, P[:, half, step % HALF, PW * g:PW * (g + 1)],
                                                    BD[:, s, step, :, 0:LS[g] + 1], start=True, stop=True)
                        if g == 0:
                            last.then_inc(c0_done, 1)
                    last.then_inc(c12_done, 1)

            def row_sums(n):
                pe.wait_ge(e_used, 2 * n + 2)
                for s in range(2):
                    last = nc.tensor.transpose(pG[0:F, s * TILE:(s + 1) * TILE], S[:, s, :], ident[:])
                last.then_inc(st_psum, 1)

            def z_rows(n):
                pe.wait_ge(c0_out, QUADS_BLK * (n + 1))
                pe.wait_ge(c12_out, QUADS_BLK * (n + 1))
                pe.wait_ge(st_out, n + 1)
                moving = [(slot, CS0, slot) for slot in range(SLOT0[1])]
                moving += [(slot, CS12, slot - SLOT0[1]) for slot in range(SLOT0[1], SLOTS)]
                z1 = [m for m in moving if m[0] in SLOT0]
                z2 = [m for m in moving if m[0] not in SLOT0]
                for x, (slot, cs, l) in enumerate(z1):
                    r = PN[group_of_slot(slot)]
                    nc.tensor.matmul(pZ[:, 0:BLOCK], TW[0:r, slot, :], cs[0:r, l, :], start=(x == 0),
                                     stop=(x == len(z1) - 1))
                for x, (slot, cs, l) in enumerate(z2):
                    r = PN[group_of_slot(slot)]
                    nc.tensor.matmul(pZ[:, BLOCK:2 * BLOCK], TW[0:r, slot, :], cs[0:r, l, :], start=(x == 0), stop=False)
                nc.tensor.matmul(pZ[:, BLOCK:2 * BLOCK], VT[:], ST[:], start=False, stop=True).then_inc(z_psum, 1)

            def mlp1(n, dense_cols):
                pe.wait_ge(z_out, n + 1)
                for c in range(N1 // 128):
                    o = pH[c // 2][:, BLOCK * (c % 2):BLOCK * (c % 2 + 1)]
                    w = slice(128 * c, 128 * (c + 1))
                    nc.tensor.matmul(o, A1[:, 0, w], ZT[:, 0, :], start=True, stop=False)
                    nc.tensor.matmul(o, A1[:, 1, w], ZT[:, 1, :], start=False, stop=False)
                    last = nc.tensor.matmul(o, A1d[:, w], dense_cols, start=False, stop=True)
                    if c % 2:
                        last.then_inc(h1_psum, 1)

            def mlp2(n):
                pe.wait_ge(h1_out, 2 * n + 2)
                for d in range(N2 // 128):
                    for c in range(N1 // 128):
                        last = nc.tensor.matmul(pG[:, BLOCK * d:BLOCK * (d + 1)], A2[:, c, 128 * d:128 * (d + 1)],
                                                H1T[:, c, :], start=(c == 0), stop=(c == N1 // 128 - 1))
                last.then_inc(h2_psum, 1)

            def mlp3(n):
                pe.wait_ge(h2_out, n + 1)
                for d in range(N2 // 128):
                    last = nc.tensor.matmul(pH[0][0:1, 0:BLOCK], cols[:, 6 + d:7 + d], H2T[:, d, :],
                                            start=(d == 0), stop=(d == N2 // 128 - 1))
                last.then_inc(y_psum, 1)

            def blk(n, first):
                tile(n, 0, first)
                if not first:
                    mlp1(n - 1, densT[:, bass.ds((n - 1) * BLOCK, BLOCK)])
                tile(n, 1, first)
                if not first:
                    mlp2(n - 1)
                z_rows(n)
                if not first:
                    mlp3(n - 1)

            pe.wait_ge(top_loaded, 16 * 3)
            blk(0, True)
            with pe.Fori(1, NBLK) as n:
                blk(n, False)
            pe.wait_ge(y_out, NBLK - 1)
            mlp1(NBLK - 1, densT[:, (NBLK - 1) * BLOCK:B])
            mlp2(NBLK - 1)
            mlp3(NBLK - 1)


_TABLES = [f"tbl_{f}" for f in range(26)]
_OTHERS = ["dense_ctx", "ids", "W_top1", "b_top1", "W_top2", "b_top2", "W_top3",
           "L0_rec_W1", "L0_rec_b1", "L0_rec_W2", "L0_rec_b2"]


def kernel(**inputs):
    import numpy as _np
    import concourse.bacc as _bacc
    from concourse import mybir as _mybir
    from concourse.bass_utils import run_bass_kernel_spmd as _run

    nc = _bacc.Bacc("TRN2", target_bir_lowering=False, num_devices=1)
    arrays, aps = {}, {}
    for name in _TABLES + _OTHERS:
        a = _np.ascontiguousarray(inputs[name])
        arrays[f"in_{name}"] = a
        aps[name] = nc.dram_tensor(f"in_{name}", a.shape, _mybir.dt.from_np(a.dtype), kind="ExternalInput").ap()
    y = nc.dram_tensor("out_y", (1024, 1), _mybir.dt.float32, kind="ExternalOutput").ap()
    o = {n: aps[n] for n in _OTHERS}
    tower_kernel(nc, o["dense_ctx"], o["ids"], [aps[t] for t in _TABLES], o["W_top1"], o["b_top1"], o["W_top2"],
                 o["b_top2"], o["W_top3"], o["L0_rec_W1"], o["L0_rec_b1"], o["L0_rec_W2"], o["L0_rec_b2"], y)
    r = _run(nc, [arrays], core_ids=[0])
    return r.results[0]["out_y"]
```

```python
from contextlib import ExitStack

import concourse.bass as bass
from concourse import mybir

F32 = mybir.dt.float32
I32 = mybir.dt.int32
U32 = mybir.dt.uint32
ALU = mybir.AluOpType
ACT = mybir.ActivationFunctionType

B = 1024
F = 26
K = 32
H = 128
DC = 16
N1 = 512
N2 = 256
TILE = 128
NT = B // TILE
Q = TILE // K
NB = K
QUAD = 4
OCT = 8
QUADS = NB // QUAD
OCTS = NB // OCT
BLOCK = 2 * TILE
NBLK = B // BLOCK

A = 18
T = 13
NBF = F - A


def first(y):
    return 0 if y < A else A


def group(y):
    return 1 if T <= y < A else 2


G1_PAIRS = sum(y + 1 for y in range(T, A))
G1_ROWS = G1_PAIRS + F
G2_ROWS = sum(y - first(y) + 1 for y in range(F) if group(y) == 2)
ROW = [sum(v - first(v) + 1 for v in range(y) if group(v) == group(y)) for y in range(F)]
PCOLS = G1_ROWS + G2_ROWS
L2 = F + 1
L1 = F - T + 1
CROSS = 4
S2 = L1
SLIN = L1 + L2
SCROSS = SLIN + 1
SLOTS = SCROSS + NBF // CROSS
CSLOTS = L1 + L2
ONES = [None, L1 - 1, S2 + L2 - 1]
PW = G2_ROWS
LAST_PIECES = 2

CUT = 13
MA = CUT * F
MB = MA + (F - CUT) * (F - CUT)
MW = MB + 1


def at(i, j):
    return F * i + j if i < CUT else MA + (F - CUT) * (i - CUT) + (j - CUT)


def step_i(i):
    return F if i < CUT else F - CUT


def parts(lo, hi):
    return [(u, v) for u, v in ((lo, min(hi, CUT)), (max(lo, CUT), hi)) if u < v]


def tower_kernel(nc, dense, ids, tables, wt1, bt1, wt2, bt2, wt3, cw1, cb1, cw2, cb2, out):
    with ExitStack() as ctx:
        def sb(name, shape, dt=F32):
            return ctx.enter_context(nc.sbuf_tensor(name, shape, dt))

        def bank(name):
            return ctx.enter_context(nc.psum_tensor(name, [128, 512], F32))

        def sem(name):
            return ctx.enter_context(nc.semaphore(name))

        CS_N = CSLOTS * TILE
        P_N = NB * PCOLS
        BD_N = NB * Q * L2
        XT_N = F * NB
        late, end = {}, 2 * CS_N
        for name, n in (("P", P_N), ("BD", BD_N), ("XT", XT_N), ("H1T", N1 // 128 * BLOCK),
                        ("H2T", N2 // 128 * BLOCK), ("ZT", 2 * BLOCK)):
            late[name] = (end, end + n)
            end += n
        M0, TC0 = CS_N, CS_N + F * MW
        arena = sb("arena", [128, max(end, TC0 + SLOTS * PW)])

        def cut(name, pattern, **sizes):
            return arena[:, late[name][0]:late[name][1]].rearrange(pattern, **sizes)

        CS = arena[:, 0:2 * CS_N].rearrange("p (s l b) -> p s l b", s=2, b=TILE)
        M = arena[:, M0:TC0].rearrange("p (l c) -> p l c", c=MW)
        Tc = arena[:, TC0:TC0 + SLOTS * PW].rearrange("p (s c) -> p s c", c=PW)
        W2nat = arena[:, TC0:TC0 + H * F].rearrange("p (i l) -> p i l", l=F)
        H1T = cut("H1T", "p (c b) -> p c b", b=BLOCK)
        H2T = cut("H2T", "p (c b) -> p c b", b=BLOCK)
        ZT = cut("ZT", "p (c b) -> p c b", b=BLOCK)
        P = [sb("P0", [128, NB, PCOLS])[:], cut("P", "p (i c) -> p i c", c=PCOLS)]
        BD = [sb("BD0", [128, NB, Q, L2])[:], cut("BD", "p (i q l) -> p i q l", q=Q, l=L2)]
        XT = [sb("XT0", [128, F, NB])[:], cut("XT", "p (f i) -> p f i", i=NB)]

        W2T = sb("W2T", [128, F, H])
        E = sb("E", [128, 2, F, K])
        TW = sb("TW", [PW, SLOTS, H])
        GX = sb("GX", [CROSS * A, NBF // CROSS, BLOCK])
        W1raw = sb("W1raw", [128, F, F])
        W1s = sb("W1s", [128, MW])
        ident = sb("ident", [128, 128])
        ids_all = sb("ids_all", [128, NT, F], I32)
        ids_now = sb("ids_now", [128, 2, F], I32)
        rows = sb("rows", [10, 128])
        cols = sb("cols", [128, 10])
        kb = sb("kb", [128, 2])
        densN = sb("densN", [128, NT, DC])
        densT = sb("densT", [DC, B])
        A1 = sb("A1", [128, 2, N1])
        A1d = sb("A1d", [DC, N1])
        A2 = sb("A2", [128, N1 // 128, N2])
        Y = W2T[0:1, 0:B // H, :].rearrange("p l h -> p (l h)")

        pC2 = [bank("pC2a"), bank("pC2b")]
        pC1 = [bank("pC1a"), bank("pC1b")]
        pZ = bank("pZ")
        pH = [bank("pHa"), bank("pHb")]
        pG = bank("pG")

        ids_loaded = sem("ids_loaded")
        w1_loaded = sem("w1_loaded")
        w2_loaded = sem("w2_loaded")
        rows_loaded = sem("rows_loaded")
        dense_loaded = sem("dense_loaded")
        top_loaded = sem("top_loaded")
        ident_zero = sem("ident_zero")
        ident_ready = sem("ident_ready")
        ids_staged = sem("ids_staged")
        gathers_begun = sem("gathers_begun")
        gathered = [sem("gathered_even"), sem("gathered_odd")]
        zeroed = sem("zeroed")
        w1_step = sem("w1_step")
        pre_psum = sem("pre_psum")
        pre_out = sem("pre_out")
        tc_step = sem("tc_step")
        xt_ready = sem("xt_ready")
        bd_ready = sem("bd_ready")
        p_ready = sem("p_ready")
        c2_done = sem("c2_done")
        c1_done = sem("c1_done")
        c2_out = sem("c2_out")
        c1_out = sem("c1_out")
        gx_ready = sem("gx_ready")
        z_psum = sem("z_psum")
        z_out = sem("z_out")
        h1_psum = sem("h1_psum")
        h1_out = sem("h1_out")
        h2_psum = sem("h2_psum")
        h2_out = sem("h2_out")
        y_psum = sem("y_psum")
        y_out = sem("y_out")
        stored = sem("stored")

        four = lambda n: [list(range(x, min(x + 4, n))) for x in range(0, n, 4)]
        prep1 = [("cols", [0])] + [("w2t", g) for g in four(F)] + [("m", [l]) for l in range(F)]
        prep1 += [("dense", g) for g in four(NT)]
        prep2 = [("tw", g) for g in four(SLOTS)]
        prep = prep1 + prep2
        BANKS1 = [pC2[0], pC2[1], pC1[0], pC1[1], pZ, pH[0], pH[1], pG]
        BANKS2 = [pZ, pH[0], pH[1], pG]
        N_PREP1 = len(prep1)
        N_PREP = len(prep)
        W2T_OUT = 1 + len(four(F))
        M_OUT = W2T_OUT + F

        def prep_bank(i):
            return BANKS1[i % len(BANKS1)] if i < N_PREP1 else BANKS2[(i - N_PREP1) % len(BANKS2)]

        block = ctx.enter_context(nc.Block())

        @block.sync
        def _(sp):
            sp.dma_start(ids_all[:], ids.rearrange("(t p) f -> p t f", p=TILE)).then_inc(ids_loaded, 16)
            sp.dma_start(W2nat, cw2).then_inc(w2_loaded, 16)
            sp.dma_start(W1raw[:], cw1).then_inc(w1_loaded, 16)
            sp.dma_start(rows[0:4, :], bt1.rearrange("(a b) -> a b", b=128)).then_inc(rows_loaded, 16)
            sp.dma_start(rows[4:6, :], bt2.rearrange("(a b) -> a b", b=128)).then_inc(rows_loaded, 16)
            sp.dma_start(rows[6:8, :], wt3.rearrange("(a b) o -> a (b o)", b=128)).then_inc(rows_loaded, 16)
            sp.dma_start(rows[8:9, :], cb1.rearrange("(a b) -> a b", a=1)).then_inc(rows_loaded, 16)
            sp.dma_start(rows[9:10, :], cb2.rearrange("(a b) -> a b", a=1)).then_inc(rows_loaded, 16)
            sp.dma_start(densN[:], dense.rearrange("(t p) f -> p t f", p=TILE)).then_inc(dense_loaded, 16)
            sp.dma_start(A1[:], wt1[0:2 * H, :].rearrange("(c p) n -> p c n", p=128)).then_inc(top_loaded, 16)
            sp.dma_start(A1d[:], wt1[2 * H:2 * H + DC, :]).then_inc(top_loaded, 16)
            sp.dma_start(A2[:], wt2.rearrange("(c p) n -> p c n", p=128)).then_inc(top_loaded, 16)

            def cross(n, begin):
                sp.wait_ge(c1_out, 2 * OCTS * (n + 1))
                if not begin:
                    sp.wait_ge(z_psum, n)
                for y in range(NBF):
                    sp.dma_start(GX[A * (y % CROSS):A * (y % CROSS + 1), y // CROSS, :].rearrange("p (s b) -> p s b", s=2),
                                 CS[G1_PAIRS:G1_PAIRS + A, :, A - T + y, :]).then_inc(gx_ready, 16)

            cross(0, True)
            with sp.Fori(1, NBLK) as n:
                cross(n, False)
            sp.wait_ge(y_out, NBLK)
            sp.dma_start(out.rearrange("b o -> o b"), Y).then_inc(stored, 16)
            sp.wait_ge(stored, 16)

        @block.gpsimd
        def _(pool):
            nc.gpsimd.memset(ident[:], 0.0).then_inc(ident_zero, 1)
            pool.wait_ge(ident_zero, 1)
            nc.gpsimd.affine_select(out=ident[:], in_=ident[:], compare_op=ALU.not_equal, fill=1.0, base=0,
                                    pattern=[[-1, 128]], channel_multiplier=1).then_inc(ident_ready, 1)
            pool.wait_ge(ids_loaded, 16)

            def tile(n, s, begin):
                if not begin:
                    pool.wait_ge(gathered[s], 16 * F * n)
                nc.gpsimd.tensor_copy(ids_now[:, s, :],
                                      ids_all[:, bass.ds(2 * n + s, 1), :].rearrange("p o f -> p (o f)")
                                      ).then_inc(ids_staged, 1)
                pool.wait_ge(ids_staged, 2 * n + s + 1)
                if not begin:
                    pool.wait_ge(xt_ready, 2 * n + s - 1)
                pool.sem_inc(gathers_begun, 1)
                for f in range(F):
                    nc.gpsimd.indirect_dma_start(
                        out=E[:, s, f, :], out_offset=None, in_=tables[f],
                        in_offset=bass.IndirectOffsetOnAxis(ap=ids_now[:, s, f:f + 1].bitcast(U32), axis=0),
                    ).then_inc(gathered[s], 16)

            for s in range(2):
                tile(0, s, True)
            with pool.Fori(1, NBLK) as n:
                for s in range(2):
                    tile(n, s, False)

        @block.vector
        def _(dve):
            def clear_bd(s, before):
                nc.vector.memset(BD[s], 0.0).then_inc(zeroed, 1)
                dve.wait_ge(zeroed, before + 1)
                for q in range(Q):
                    nc.vector.memset(BD[s][K * q:K * q + K, :, q, F], 1.0).then_inc(zeroed, 1)

            clear_bd(0, 0)
            dve.wait_ge(w1_loaded, 16)
            w1t = W1raw[:].rearrange("p i j -> p j i")
            nc.vector.tensor_tensor(W1s[:, 0:MA].rearrange("p (i j) -> p i j", j=F), W1raw[:, 0:CUT, :],
                                    w1t[:, 0:CUT, :], ALU.add).then_inc(w1_step, 1)
            nc.vector.tensor_tensor(W1s[:, MA:MB].rearrange("p (i j) -> p i j", j=F - CUT), W1raw[:, CUT:F, CUT:F],
                                    w1t[:, CUT:F, CUT:F], ALU.add).then_inc(w1_step, 1)
            dve.wait_ge(w1_step, 2)
            flat = W1raw[:].rearrange("p i j -> p (i j)")
            nc.vector.tensor_copy(W1s[:, 0:MA:F + 1], flat[:, 0:MA:F + 1]).then_inc(w1_step, 1)
            nc.vector.tensor_copy(W1s[:, MA:MB:F - CUT + 1], flat[:, (F + 1) * CUT::F + 1]).then_inc(w1_step, 1)
            dve.wait_ge(pre_out, 1)
            nc.vector.tensor_copy(W1s[:, MB:MW], cols[:, 8:9]).then_inc(w1_step, 1)
            nc.vector.tensor_scalar(kb[:], cols[:, 8:10], float(K), None, ALU.mult).then_inc(w1_step, 1)
            dve.wait_ge(pre_out, W2T_OUT)
            nc.vector.memset(Tc, 0.0).then_inc(zeroed, 1)
            dve.wait_ge(zeroed, 2 + Q)
            dve.wait_ge(w1_step, 6)
            for y in range(F):
                for u, v in parts(first(y), y + 1):
                    r = ROW[y] + u - first(y)
                    nc.vector.tensor_copy(Tc[:, ONES[group(y)], r:r + v - u],
                                          W1s[:, at(u, y):at(v - 1, y) + 1:step_i(u)])
                for u, v in parts(0, A) if y >= A else []:
                    r = A * ((y - A) % CROSS) + u
                    nc.vector.tensor_copy(Tc[:, SCROSS + (y - A) // CROSS, r:r + v - u],
                                          W1s[:, at(u, y):at(v - 1, y) + 1:step_i(u)])

            def m_view(offset, *dims):
                return bass.AP(tensor=M.tensor, offset=M.offset + offset, ap=[list(M.ap[0]), *map(list, dims)])

            def fold():
                dve.wait_ge(pre_out, M_OUT)
                nc.vector.tensor_copy(Tc[:, SLIN, G1_PAIRS:G1_ROWS], M[:, :, MB])
                for y in range(F):
                    slot = (lambda z: S2 + z) if group(y) == 2 else (lambda z: z - T)
                    for u, v in parts(first(y), y + 1):
                        r, n = ROW[y] + u - first(y), v - u
                        last = nc.vector.tensor_copy(Tc[:, slot(y), r:r + n],
                                                     m_view(y * MW + at(u, y), (step_i(u), n)))
                        if y < F - 1:
                            last = nc.vector.tensor_tensor(
                                Tc[:, slot(y + 1):slot(F - 1) + 1, r:r + n],
                                m_view((y + 1) * MW + at(u, y), (MW, F - 1 - y), (step_i(u), n)),
                                m_view(y * MW + at(u, y + 1), (1, F - 1 - y), (step_i(u), n)), ALU.add)
                    for u, v in parts(0, A) if y >= A else []:
                        n = y - A + 1
                        last = nc.vector.tensor_tensor(
                            Tc[:, S2 + u:S2 + v, ROW[y]:ROW[y] + n],
                            m_view(u * MW + at(A, y), (MW, v - u), (step_i(A), n)),
                            m_view(A * MW + at(u, y), (step_i(u), v - u), (MW, n)), ALU.add)
                last.then_inc(tc_step, 1)
                dve.wait_ge(tc_step, 1)
                for y in range(F):
                    slot = (lambda z: S2 + z) if group(y) == 2 else (lambda z: z - T)
                    n = y - first(y)
                    if n == 0:
                        continue
                    t = Tc[:, slot(y):slot(F - 1) + 1, ROW[y]:ROW[y] + n]
                    last = nc.vector.tensor_tensor(
                        t, t, m_view(first(y) * MW + at(y, y), (1, F - y), (MW, n)), ALU.add)
                    for u, v in parts(0, A) if y >= A else []:
                        t = Tc[:, S2 + u:S2 + v, ROW[y]:ROW[y] + n]
                        last = nc.vector.tensor_tensor(
                            t, t, m_view(y * MW + at(u, A), (step_i(u), v - u), (1, n)), ALU.add)
                last.then_inc(tc_step, 1)

            def tile(n, s, begin, pieces=1):
                dve.wait_ge(gathered[s], 16 * F * (n + 1))
                nc.vector.transpose(XT[s].rearrange("p f i -> p (f i)"),
                                    E[:, s].rearrange("p f k -> p (f k)")).then_inc(xt_ready, 1)
                dve.wait_ge(xt_ready, 2 * n + s + 1)
                if not begin:
                    dve.wait_ge(c1_done, OCTS * (2 * n + s - 1))
                for q in range(Q):
                    r = slice(K * q, K * q + K)
                    last = nc.vector.tensor_copy(BD[s][r, :, q, 0:F], XT[s][r].rearrange("p f i -> p i f"))
                last.then_inc(bd_ready, 1)
                for i0 in range(0, NB, NB // pieces):
                    i1 = i0 + NB // pieces
                    x_if = XT[s][:, :, i0:i1].rearrange("p f i -> p i f")
                    nc.vector.tensor_copy(P[s][:, i0:i1, G1_PAIRS:G1_ROWS], x_if)
                    for y in range(F):
                        r = ROW[y] + (G1_ROWS if group(y) == 2 else 0)
                        w = y - first(y) + 1
                        last = nc.vector.tensor_tensor(
                            P[s][:, i0:i1, r:r + w], x_if[:, :, first(y):y + 1],
                            XT[s][:, y, i0:i1].unsqueeze(2).broadcast_to([128, i1 - i0, w]), ALU.mult)
                    last.then_inc(p_ready, 1)

            tile(0, 0, True)
            fold()
            dve.wait_ge(pre_psum, N_PREP)
            clear_bd(1, 2 + Q)
            dve.wait_ge(zeroed, 3 + 2 * Q)
            tile(0, 1, True)
            with dve.Fori(1, NBLK - 1) as n:
                for s in range(2):
                    tile(n, s, False)
            tile(NBLK - 1, 0, False)
            tile(NBLK - 1, 1, False, pieces=LAST_PIECES)

        @block.scalar
        def _(act):
            def empty(lo, hi):
                for i in range(lo, hi):
                    kind, g = prep[i]
                    src = prep_bank(i)
                    act.wait_ge(pre_psum, i + 1)
                    if kind == "cols":
                        last = nc.scalar.copy(cols[:], src[:, 0:10])
                    elif kind == "w2t":
                        last = nc.scalar.copy(W2T[:, g[0]:g[-1] + 1, :],
                                              src[:, 0:len(g) * H].rearrange("p (l h) -> p l h", h=H))
                    elif kind == "m":
                        last = nc.scalar.copy(M[:, g[0], :], src[:, 0:MW])
                    elif kind == "dense":
                        for x, t in enumerate(g):
                            last = nc.scalar.copy(
                                densT[:, t * TILE:(t + 1) * TILE].rearrange("p (i q) -> p q i", q=Q),
                                src[0:DC, x * TILE:(x + 1) * TILE].rearrange("p (q i) -> p q i", q=Q))
                    else:
                        last = nc.scalar.copy(TW[:, g[0]:g[-1] + 1, :],
                                              src[0:PW, 0:len(g) * H].rearrange("p (s h) -> p s h", h=H))
                    last.then_inc(pre_out, 1)

            def tile(n, s):
                for j in range(QUADS):
                    act.wait_ge(c2_done, QUADS * (2 * n + s) + j + 1)
                    nc.scalar.copy(CS[0:G2_ROWS, s, S2:CSLOTS, Q * QUAD * j:Q * QUAD * (j + 1)].rearrange("p l b -> p b l"),
                                   pC2[j % 2][0:G2_ROWS, 0:QUAD * Q * L2].rearrange("p (b l) -> p b l", l=L2)
                                   ).then_inc(c2_out, 1)
                    if j % 2:
                        o = j // 2
                        act.wait_ge(c1_done, OCTS * (2 * n + s) + o + 1)
                        nc.scalar.copy(CS[0:G1_ROWS, s, 0:S2, Q * OCT * o:Q * OCT * (o + 1)].rearrange("p l b -> p b l"),
                                       pC1[o % 2][0:G1_ROWS, 0:OCT * Q * L1].rearrange("p (b l) -> p b l", l=L1)
                                       ).then_inc(c1_out, 1)

            def mlp1(n):
                for c in range(2):
                    act.wait_ge(h1_psum, 2 * n + c + 1)
                    for d in range(2):
                        last = nc.scalar.activation(H1T[:, 2 * c + d, :], pH[c][:, BLOCK * d:BLOCK * (d + 1)], ACT.Relu,
                                                    bias=cols[:, 2 * c + d:2 * c + d + 1])
                    last.then_inc(h1_out, 1)

            def mlp2(n):
                act.wait_ge(h2_psum, n + 1)
                for d in range(2):
                    last = nc.scalar.activation(H2T[:, d, :], pG[:, BLOCK * d:BLOCK * (d + 1)], ACT.Relu,
                                                bias=cols[:, 4 + d:5 + d])
                last.then_inc(h2_out, 1)

            def mlp3(n):
                act.wait_ge(y_psum, n + 1)
                for s in range(2):
                    last = nc.scalar.copy(
                        Y[:, bass.ds(n * BLOCK + s * TILE, TILE)].rearrange("p (q i) -> p i q", q=Q),
                        pH[0][0:1, s * TILE:(s + 1) * TILE].rearrange("p (i q) -> p i q", q=Q))
                last.then_inc(y_out, 1)

            def z_rows(n):
                act.wait_ge(z_psum, n + 1)
                for d in range(2):
                    last = nc.scalar.activation(ZT[:, d, :], pZ[:, BLOCK * d:BLOCK * (d + 1)], ACT.Identity,
                                                bias=kb[:, d:d + 1])
                last.then_inc(z_out, 1)

            empty(0, N_PREP1)
            tile(0, 0)
            empty(N_PREP1, N_PREP)
            tile(0, 1)
            z_rows(0)
            with act.Fori(1, NBLK) as n:
                tile(n, 0)
                mlp1(n - 1)
                tile(n, 1)
                mlp2(n - 1)
                z_rows(n)
                mlp3(n - 1)
            mlp1(NBLK - 1)
            mlp2(NBLK - 1)
            mlp3(NBLK - 1)

        @block.tensor
        def _(pe):
            def fill(lo, hi):
                for i in range(lo, hi):
                    kind, g = prep[i]
                    dst = prep_bank(i)
                    back = i - (len(BANKS1) if i < N_PREP1 else len(BANKS2))
                    if back >= 0:
                        pe.wait_ge(pre_out, back + 1)
                    if kind == "cols":
                        pe.wait_ge(rows_loaded, 16 * 5)
                        last = nc.tensor.transpose(dst[:, 0:10], rows[:], ident[0:10, 0:10])
                    elif kind == "w2t":
                        pe.wait_ge(w2_loaded, 16)
                        for x, l in enumerate(g):
                            last = nc.tensor.transpose(dst[:, x * H:(x + 1) * H], W2nat[:, :, l], ident[:])
                    elif kind == "m":
                        if g[0] == 0:
                            pe.wait_ge(w1_step, 5)
                            pe.wait_ge(pre_out, W2T_OUT)
                        last = nc.tensor.matmul(dst[:, 0:MW], W2T[:, g[0], :], W1s[:], start=True, stop=True)
                    elif kind == "dense":
                        pe.wait_ge(dense_loaded, 16)
                        for x, t in enumerate(g):
                            last = nc.tensor.transpose(dst[0:DC, x * TILE:(x + 1) * TILE], densN[:, t, :], ident[:])
                    else:
                        pe.wait_ge(tc_step, 2)
                        for x, s in enumerate(g):
                            last = nc.tensor.transpose(dst[0:PW, x * H:(x + 1) * H], Tc[:, s, :], ident[:])
                    last.then_inc(pre_psum, 1)

            def tile(n, s, begin, pieces=1):
                t = 2 * n + s
                pe.wait_ge(bd_ready, t + 1)
                for i in range(NB):
                    if i % (NB // pieces) == 0:
                        pe.wait_ge(p_ready, t + i // (NB // pieces) + 1)
                    j, o = i // QUAD, i // OCT
                    if i % QUAD == 0 and not (begin and s == 0 and j < 2):
                        pe.wait_ge(c2_out, QUADS * t + j - 1)
                    at2 = Q * L2 * (i % QUAD)
                    mm = nc.tensor.matmul(pC2[j % 2][0:G2_ROWS, at2:at2 + Q * L2].rearrange("p (q l) -> p q l", l=L2),
                                          P[s][:, i, G1_ROWS:PCOLS], BD[s][:, i, :, :], start=True, stop=True)
                    if i % QUAD == QUAD - 1:
                        mm.then_inc(c2_done, 1)
                    if i % OCT == 0 and not (begin and s == 0 and o < 2):
                        pe.wait_ge(c1_out, OCTS * t + o - 1)
                    at1 = Q * L1 * (i % OCT)
                    mm = nc.tensor.matmul(pC1[o % 2][0:G1_ROWS, at1:at1 + Q * L1].rearrange("p (q l) -> p q l", l=L1),
                                          P[s][:, i, 0:G1_ROWS], BD[s][:, i, :, T:L2], start=True, stop=True)
                    if i % OCT == OCT - 1:
                        mm.then_inc(c1_done, 1)

            def z_rows(n):
                pe.wait_ge(c2_out, QUADS * 2 * (n + 1))
                pe.wait_ge(c1_out, OCTS * 2 * (n + 1))
                z1, z2 = pZ[:, 0:BLOCK], pZ[:, BLOCK:2 * BLOCK]

                def mm(z, rows_, slot, cs, **flags):
                    return nc.tensor.matmul(z.rearrange("p (s b) -> p s b", s=2), TW[0:rows_, slot, :],
                                            CS[0:rows_, :, cs, :], **flags)

                mm(z2, G1_ROWS, SLIN, ONES[1], start=True, stop=False)
                for l in range(L1 - 1):
                    mm(z2, G1_PAIRS, l, l, start=False, stop=False)
                for l in range(L2 - 1):
                    mm(z2, G2_ROWS, S2 + l, S2 + l, start=False, stop=(l == L2 - 2))
                mm(z1, G1_PAIRS, ONES[1], ONES[1], start=True, stop=False)
                mm(z1, G2_ROWS, ONES[2], ONES[2], start=False, stop=False)
                pe.wait_ge(gx_ready, 16 * NBF * (n + 1))
                for c in range(NBF // CROSS):
                    last = nc.tensor.matmul(z1, TW[0:CROSS * A, SCROSS + c, :], GX[:, c, :], start=False,
                                            stop=(c == NBF // CROSS - 1))
                last.then_inc(z_psum, 1)

            def mlp1(n, dense_cols):
                pe.wait_ge(z_out, n + 1)
                for c in range(N1 // 128):
                    o = pH[c // 2][:, BLOCK * (c % 2):BLOCK * (c % 2 + 1)]
                    w = slice(128 * c, 128 * (c + 1))
                    nc.tensor.matmul(o, A1[:, 0, w], ZT[:, 0, :], start=True, stop=False)
                    nc.tensor.matmul(o, A1[:, 1, w], ZT[:, 1, :], start=False, stop=False)
                    last = nc.tensor.matmul(o, A1d[:, w], dense_cols, start=False, stop=True)
                    if c % 2:
                        last.then_inc(h1_psum, 1)

            def mlp2(n):
                pe.wait_ge(h1_out, 2 * n + 2)
                for d in range(N2 // 128):
                    for c in range(N1 // 128):
                        last = nc.tensor.matmul(pG[:, BLOCK * d:BLOCK * (d + 1)], A2[:, c, 128 * d:128 * (d + 1)],
                                                H1T[:, c, :], start=(c == 0), stop=(c == N1 // 128 - 1))
                last.then_inc(h2_psum, 1)

            def mlp3(n):
                pe.wait_ge(h2_out, n + 1)
                for d in range(N2 // 128):
                    last = nc.tensor.matmul(pH[0][0:1, 0:BLOCK], cols[:, 6 + d:7 + d], H2T[:, d, :],
                                            start=(d == 0), stop=(d == N2 // 128 - 1))
                last.then_inc(y_psum, 1)

            def blk(n, pieces=1):
                tile(n, 0, False)
                mlp1(n - 1, densT[:, bass.ds((n - 1) * BLOCK, BLOCK)])
                tile(n, 1, False, pieces)
                mlp2(n - 1)
                z_rows(n)
                mlp3(n - 1)

            pe.wait_ge(ident_ready, 1)
            fill(0, N_PREP1)
            pe.wait_ge(pre_out, N_PREP1)
            tile(0, 0, True)
            fill(N_PREP1, N_PREP)
            tile(0, 1, True)
            pe.wait_ge(pre_out, N_PREP)
            pe.wait_ge(top_loaded, 16 * 3)
            z_rows(0)
            with pe.Fori(1, NBLK - 1) as n:
                blk(n)
            blk(NBLK - 1, LAST_PIECES)
            pe.wait_ge(y_out, NBLK - 1)
            mlp1(NBLK - 1, densT[:, (NBLK - 1) * BLOCK:B])
            mlp2(NBLK - 1)
            mlp3(NBLK - 1)


_TABLES = [f"tbl_{f}" for f in range(26)]
_OTHERS = ["dense_ctx", "ids", "W_top1", "b_top1", "W_top2", "b_top2", "W_top3",
           "L0_rec_W1", "L0_rec_b1", "L0_rec_W2", "L0_rec_b2"]


def kernel(**inputs):
    import numpy as _np
    import concourse.bacc as _bacc
    from concourse import mybir as _mybir
    from concourse.bass_utils import run_bass_kernel_spmd as _run

    nc = _bacc.Bacc("TRN2", target_bir_lowering=False, num_devices=1)
    arrays, aps = {}, {}
    for name in _TABLES + _OTHERS:
        a = _np.ascontiguousarray(inputs[name])
        arrays[f"in_{name}"] = a
        aps[name] = nc.dram_tensor(f"in_{name}", a.shape, _mybir.dt.from_np(a.dtype), kind="ExternalInput").ap()
    y = nc.dram_tensor("out_y", (1024, 1), _mybir.dt.float32, kind="ExternalOutput").ap()
    o = {n: aps[n] for n in _OTHERS}
    tower_kernel(nc, o["dense_ctx"], o["ids"], [aps[t] for t in _TABLES], o["W_top1"], o["b_top1"], o["W_top2"],
                 o["b_top2"], o["W_top3"], o["L0_rec_W1"], o["L0_rec_b1"], o["L0_rec_W2"], o["L0_rec_b2"], y)
    r = _run(nc, [arrays], core_ids=[0])
    return r.results[0]["out_y"]
```

```python
from contextlib import ExitStack

import concourse.bass as bass
from concourse import mybir

F32 = mybir.dt.float32
I32 = mybir.dt.int32
U32 = mybir.dt.uint32
ALU = mybir.AluOpType
ACT = mybir.ActivationFunctionType

B = 1024
F = 26
K = 32
H = 128
DC = 16
N1 = 512
N2 = 256
TILE = 128
NT = B // TILE
Q = TILE // K
NB = K
QUAD = 4
QUADS = NB // QUAD
NPAIR = NT // 2

A = 14
T = 9
NBF = F - A
CHUNKS = [(0, A), (A, 24), (24, F)]


def first(y):
    return 0 if y < A else A


def group(y):
    return 1 if T <= y < A else 2


G1_PAIRS = sum(y + 1 for y in range(T, A))
G1_ROWS = G1_PAIRS + A
G2_PAIRS = sum(y - first(y) + 1 for y in range(F) if group(y) == 2)
G2_ROWS = G2_PAIRS + 1
ROW = [sum(v - first(v) + 1 for v in range(y) if group(v) == group(y)) for y in range(F)]
PCOLS = G1_ROWS + G2_ROWS
L2 = F + 1
L1 = F - T + 1
C1_AT = L2
CSLOTS = L2 + L1
ONES2, ONES1 = F, C1_AT + L1 - 1
CROSS = 9
CROSS_ROWS = [A * min(CROSS, NBF - c) for c in range(0, NBF, CROSS)]
ONES1_AT = CROSS_ROWS[-1]
CROSS_ROWS[-1] += G1_PAIRS
assert max(CROSS_ROWS) <= 128
N_CROSS = sum(CROSS_ROWS)
S_CROSS = L2
S_PACK = S_CROSS + len(CROSS_ROWS)
N_PACK = (L1 - 1) * G1_PAIRS
PACKS = -(-N_PACK // 128)
SLOTS = S_PACK + PACKS

CUT = 13
MA = CUT * F
MB = MA + (F - CUT) * (F - CUT)
MW = MB + 1


def at(i, j):
    return F * i + j if i < CUT else MA + (F - CUT) * (i - CUT) + (j - CUT)


def step_i(i):
    return F if i < CUT else F - CUT


def parts(lo, hi):
    return [(u, v) for u, v in ((lo, min(hi, CUT)), (max(lo, CUT), hi)) if u < v]


def tower_kernel(nc, dense, ids, tables, wt1, bt1, wt2, bt2, wt3, cw1, cb1, cw2, cb2, out):
    with ExitStack() as ctx:
        def sb(name, shape, dt=F32):
            return ctx.enter_context(nc.sbuf_tensor(name, shape, dt))

        def bank(name):
            return ctx.enter_context(nc.psum_tensor(name, [128, 512], F32))

        def sem(name):
            return ctx.enter_context(nc.semaphore(name))

        late, end = {}, 0
        for name, n in (("P", NB * PCOLS), ("XT", F * NB), ("TW", SLOTS * H), ("GP", PACKS * TILE),
                        ("GX", len(CROSS_ROWS) * TILE), ("ZT", 2 * TILE), ("H1T", N1), ("H2T", N2)):
            late[name] = (end, end + n)
            end += n
        assert F * MW <= end
        arena = sb("arena", [128, end])

        def cut(name, pattern, **sizes):
            return arena[:, late[name][0]:late[name][1]].rearrange(pattern, **sizes)

        M = arena[:, 0:F * MW].rearrange("p (l c) -> p l c", c=MW)
        TW = cut("TW", "p (s h) -> p s h", h=H)
        GP = cut("GP", "p (c b) -> p c b", b=TILE)
        GX = cut("GX", "p (c b) -> p c b", b=TILE)
        ZT = cut("ZT", "p (c b) -> p c b", b=TILE)
        H1T = cut("H1T", "p (c b) -> p c b", b=TILE)
        H2T = cut("H2T", "p (c b) -> p c b", b=TILE)
        P = [sb("P0", [128, NB, PCOLS])[:], cut("P", "p (i c) -> p i c", c=PCOLS)]
        BD = [sb("BD0", [128, NB, Q, L2])[:], sb("BD1", [128, NB, Q, L2])[:]]
        XT = [sb("XT0", [128, F, NB])[:], cut("XT", "p (f i) -> p f i", i=NB)]
        CS = sb("CS", [128, CSLOTS, TILE])
        Tc = sb("Tc", [128, SLOTS, H])[:]
        W2nat = Tc[:, 0:F, :].rearrange("p s c -> p (s c)").rearrange("p (i l) -> p i l", l=F)

        W2T = sb("W2T", [128, F, H])
        E = sb("E", [128, 2, F, K])
        packed = nc.dram_tensor("packed", (N_PACK, TILE), F32, kind="Internal").ap()
        crossed = nc.dram_tensor("crossed", (N_CROSS, TILE), F32, kind="Internal").ap()
        W1raw = sb("W1raw", [128, F, F])
        W1s = sb("W1s", [128, MW])
        ident = sb("ident", [128, 128])
        ids_all = sb("ids_all", [128, NT + 2, F], I32)
        ids_now = sb("ids_now", [128, 2, F], I32)
        rows = sb("rows", [10, 128])
        cols = sb("cols", [128, 10])
        kb = sb("kb", [128, 2])
        densN = sb("densN", [128, NT, DC])
        densT = sb("densT", [DC, B])
        A1 = sb("A1", [128, 2, N1])
        A1d = sb("A1d", [DC, N1])
        A2 = sb("A2", [128, N1 // 128, N2])
        Y = W2T[0:1, 0:B // H, :].rearrange("p l h -> p (l h)")

        pC2 = [bank("pC2a"), bank("pC2b")]
        pC1 = [bank("pC1a"), bank("pC1b"), bank("pC1c")]
        pX, pY, pZ = bank("pX"), bank("pY"), bank("pZ")
        Z = [pC1[0][:, 0:TILE], pZ[:, 0:TILE]]
        H1 = [pX, pX, pC1[1], pC1[1]]
        H2 = [pY[:, 0:TILE], pX[:, 0:TILE]]
        Y_ROW = pY[0:1, TILE:2 * TILE]

        def c_bank(banks, j):
            return banks[j % len(banks)]

        def before(banks, j):
            return len(banks) if j >= len(banks) else QUADS + j - max(i for i in range(QUADS) if i % len(banks) == j)

        ids_first = sem("ids_first")
        ids_loaded = sem("ids_loaded")
        w1_loaded = sem("w1_loaded")
        w2_loaded = sem("w2_loaded")
        rows_loaded = sem("rows_loaded")
        dense_loaded = sem("dense_loaded")
        top_loaded = sem("top_loaded")
        ident_zero = sem("ident_zero")
        ident_ready = sem("ident_ready")
        ids_staged = sem("ids_staged")
        gathers_begun = sem("gathers_begun")
        gathered = [[sem(f"gathered_{c}_{s}") for c in range(len(CHUNKS))] for s in ("even", "odd")]
        zeroed = sem("zeroed")
        w1_step = sem("w1_step")
        pre_psum = sem("pre_psum")
        pre_out = sem("pre_out")
        tc_step = sem("tc_step")
        xt_ready = sem("xt_ready")
        bd_ready = sem("bd_ready")
        p_ready = sem("p_ready")
        c2_done = sem("c2_done")
        c1_done = sem("c1_done")
        c2_out = sem("c2_out")
        c1_out = sem("c1_out")
        g_stored = sem("g_stored")
        g_back = sem("g_back")
        z_psum = sem("z_psum")
        z_out = sem("z_out")
        h1_psum = sem("h1_psum")
        h1_out = sem("h1_out")
        h2_psum = sem("h2_psum")
        h2_out = sem("h2_out")
        y_psum = sem("y_psum")
        y_out = sem("y_out")
        stored = sem("stored")

        four = lambda n: [list(range(x, min(x + 4, n))) for x in range(0, n, 4)]
        prep1 = [("cols", [0])] + [("w2t", g) for g in four(F)] + [("m", [l]) for l in range(F)]
        prep1 += [("dense", g) for g in four(NT)]
        prep2 = [("tw", g) for g in four(SLOTS)]
        prep = prep1 + prep2
        BANKS1 = [*pC2, *pC1, pX, pY, pZ]
        BANKS2 = [pX, pY, pZ]
        N_PREP1 = len(prep1)
        N_PREP = len(prep)
        W2T_OUT = 1 + len(four(F))
        M_OUT = W2T_OUT + F

        G_BACK = 16 * (2 + len(CROSS_ROWS))

        def prep_bank(i):
            return BANKS1[i % len(BANKS1)] if i < N_PREP1 else BANKS2[(i - N_PREP1) % len(BANKS2)]

        block = ctx.enter_context(nc.Block())

        @block.sync
        def _(sp):
            ids_by_tile = ids.rearrange("(t p) f -> p t f", p=TILE)
            sp.dma_start(ids_all[:, 0:2, :], ids_by_tile[:, 0:2, :]).then_inc(ids_first, 16)
            sp.dma_start(W2nat, cw2).then_inc(w2_loaded, 16)
            sp.dma_start(W1raw[:], cw1).then_inc(w1_loaded, 16)
            sp.dma_start(ids_all[:, 2:NT, :], ids_by_tile[:, 2:NT, :]).then_inc(ids_loaded, 16)
            sp.dma_start(rows[0:4, :], bt1.rearrange("(a b) -> a b", b=128)).then_inc(rows_loaded, 16)
            sp.dma_start(rows[4:6, :], bt2.rearrange("(a b) -> a b", b=128)).then_inc(rows_loaded, 16)
            sp.dma_start(rows[6:8, :], wt3.rearrange("(a b) o -> a (b o)", b=128)).then_inc(rows_loaded, 16)
            sp.dma_start(rows[8:9, :], cb1.rearrange("(a b) -> a b", a=1)).then_inc(rows_loaded, 16)
            sp.dma_start(rows[9:10, :], cb2.rearrange("(a b) -> a b", a=1)).then_inc(rows_loaded, 16)
            sp.dma_start(densN[:], dense.rearrange("(t p) f -> p t f", p=TILE)).then_inc(dense_loaded, 16)
            sp.dma_start(A1[:], wt1[0:2 * H, :].rearrange("(c p) n -> p c n", p=128)).then_inc(top_loaded, 16)
            sp.dma_start(A1d[:], wt1[2 * H:2 * H + DC, :]).then_inc(top_loaded, 16)
            sp.dma_start(A2[:], wt2.rearrange("(c p) n -> p c n", p=128)).then_inc(top_loaded, 16)

            def repack(t, begin=False):
                sp.wait_ge(c1_out, QUADS * (t + 1))
                sp.dma_start(packed.rearrange("(l r) b -> r l b", r=G1_PAIRS),
                             CS[0:G1_PAIRS, C1_AT:C1_AT + L1 - 1, :]).then_inc(g_stored, 16)
                sp.dma_start(crossed[0:NBF * A].rearrange("(l r) b -> r l b", r=A),
                             CS[G1_PAIRS:G1_ROWS, C1_AT + A - T:C1_AT + L1 - 1, :]).then_inc(g_stored, 16)
                sp.dma_start(crossed[NBF * A:N_CROSS], CS[0:G1_PAIRS, ONES1, :]).then_inc(g_stored, 16)
                sp.wait_ge(g_stored, 48 * (t + 1))
                if begin:
                    sp.wait_ge(tc_step, 2)
                whole = N_PACK // 128
                sp.dma_start(GP[:, 0:whole, :],
                             packed[0:128 * whole].rearrange("(c p) b -> p c b", p=128)).then_inc(g_back, 16)
                sp.dma_start(GP[0:N_PACK - 128 * whole, whole, :], packed[128 * whole:N_PACK]).then_inc(g_back, 16)
                for c, r in enumerate(CROSS_ROWS):
                    sp.dma_start(GX[0:r, c, :], crossed[A * CROSS * c:A * CROSS * c + r]).then_inc(g_back, 16)

            repack(0, begin=True)
            repack(1)
            with sp.Fori(1, NPAIR) as n:
                for s in range(2):
                    repack(2 * n + s)
            sp.wait_ge(y_out, NT)
            sp.dma_start(out.rearrange("b o -> o b"), Y).then_inc(stored, 16)
            sp.wait_ge(stored, 16)

        @block.gpsimd
        def _(pool):
            nc.gpsimd.memset(ident[:], 0.0).then_inc(ident_zero, 1)
            pool.wait_ge(ident_zero, 1)
            nc.gpsimd.affine_select(out=ident[:], in_=ident[:], compare_op=ALU.not_equal, fill=1.0, base=0,
                                    pattern=[[-1, 128]], channel_multiplier=1).then_inc(ident_ready, 1)
            pool.wait_ge(ids_first, 16)

            def tile(n, s, begin):
                if not begin:
                    pool.wait_ge(ids_staged, 2 * (n - 1) + s + 1)
                pool.sem_inc(gathers_begun, 1)
                for f, c in ((f, c) for c, (u, v) in enumerate(CHUNKS) for f in range(u, v)):
                    i = ids_all[:, s, f:f + 1] if begin else ids_now[:, s, f:f + 1]
                    nc.gpsimd.indirect_dma_start(
                        out=E[:, s, f, :], out_offset=None, in_=tables[f],
                        in_offset=bass.IndirectOffsetOnAxis(ap=i.bitcast(U32), axis=0),
                    ).then_inc(gathered[s][c], 16)

            for s in range(2):
                tile(0, s, True)
            with pool.Fori(1, NPAIR) as n:
                for s in range(2):
                    tile(n, s, False)

        @block.vector
        def _(dve):
            nc.vector.memset(P[0][:, :, PCOLS - 1:PCOLS], 1.0).then_inc(zeroed, 1)
            for s in range(2):
                nc.vector.memset(BD[s], 0.0).then_inc(zeroed, 1)
            nc.vector.memset(ids_all[:, NT:NT + 2, :], 0).then_inc(zeroed, 1)
            dve.wait_ge(zeroed, 4)
            for s in range(2):
                for q in range(Q):
                    nc.vector.memset(BD[s][K * q:K * q + K, :, q, F], 1.0).then_inc(zeroed, 1)
            dve.wait_ge(ids_loaded, 16)
            dve.wait_ge(w1_loaded, 16)
            w1t = W1raw[:].rearrange("p i j -> p j i")
            nc.vector.tensor_tensor(W1s[:, 0:MA].rearrange("p (i j) -> p i j", j=F), W1raw[:, 0:CUT, :],
                                    w1t[:, 0:CUT, :], ALU.add).then_inc(w1_step, 1)
            nc.vector.tensor_tensor(W1s[:, MA:MB].rearrange("p (i j) -> p i j", j=F - CUT), W1raw[:, CUT:F, CUT:F],
                                    w1t[:, CUT:F, CUT:F], ALU.add).then_inc(w1_step, 1)
            dve.wait_ge(w1_step, 2)
            flat = W1raw[:].rearrange("p i j -> p (i j)")
            nc.vector.tensor_copy(W1s[:, 0:MA:F + 1], flat[:, 0:MA:F + 1]).then_inc(w1_step, 1)
            nc.vector.tensor_copy(W1s[:, MA:MB:F - CUT + 1], flat[:, (F + 1) * CUT::F + 1]).then_inc(w1_step, 1)
            dve.wait_ge(pre_out, 1)
            nc.vector.tensor_copy(W1s[:, MB:MW], cols[:, 8:9]).then_inc(w1_step, 1)
            nc.vector.tensor_scalar(kb[:], cols[:, 8:10], float(K), None, ALU.mult).then_inc(w1_step, 1)
            dve.wait_ge(pre_out, W2T_OUT)
            nc.vector.memset(Tc, 0.0).then_inc(zeroed, 1)
            dve.wait_ge(zeroed, 5 + 2 * Q)
            dve.wait_ge(w1_step, 6)
            for y in range(F):
                for u, v in parts(first(y), y + 1):
                    r = ROW[y] + u - first(y) + (0 if group(y) == 2 else ONES1_AT)
                    nc.vector.tensor_copy(Tc[:, ONES2 if group(y) == 2 else S_PACK - 1, r:r + v - u],
                                          W1s[:, at(u, y):at(v - 1, y) + 1:step_i(u)])
                for u, v in parts(0, A) if y >= A else []:
                    r = A * ((y - A) % CROSS) + u
                    nc.vector.tensor_copy(Tc[:, S_CROSS + (y - A) // CROSS, r:r + v - u],
                                          W1s[:, at(u, y):at(v - 1, y) + 1:step_i(u)])

            def m_view(offset, *dims):
                return bass.AP(tensor=M.tensor, offset=M.offset + offset, ap=[list(M.ap[0]), *map(list, dims)])

            def t_view(y, z0, z1, r, n):
                at0, row = (0, H) if group(y) == 2 else (S_PACK * H - T * G1_PAIRS, G1_PAIRS)
                return bass.AP(tensor=Tc.tensor, offset=Tc.offset + at0 + row * z0 + r,
                               ap=[list(Tc.ap[0]), [row, z1 - z0], [1, n]])

            def fold():
                dve.wait_ge(pre_out, M_OUT)
                nc.vector.tensor_copy(Tc[:, 0:F, G2_PAIRS], M[:, :, MB])
                for y in range(F):
                    for u, v in parts(first(y), y + 1):
                        r, n = ROW[y] + u - first(y), v - u
                        last = nc.vector.tensor_copy(t_view(y, y, y + 1, r, n),
                                                     m_view(y * MW + at(u, y), (1, 1), (step_i(u), n)))
                        if y < F - 1:
                            last = nc.vector.tensor_tensor(
                                t_view(y, y + 1, F, r, n),
                                m_view((y + 1) * MW + at(u, y), (MW, F - 1 - y), (step_i(u), n)),
                                m_view(y * MW + at(u, y + 1), (1, F - 1 - y), (step_i(u), n)), ALU.add)
                    for u, v in parts(0, A) if y >= A else []:
                        n = y - A + 1
                        last = nc.vector.tensor_tensor(
                            t_view(y, u, v, ROW[y], n),
                            m_view(u * MW + at(A, y), (MW, v - u), (step_i(A), n)),
                            m_view(A * MW + at(u, y), (step_i(u), v - u), (MW, n)), ALU.add)
                last.then_inc(tc_step, 1)
                dve.wait_ge(tc_step, 1)
                for y in range(F):
                    n = y - first(y)
                    if n == 0:
                        continue
                    t = t_view(y, y, F, ROW[y], n)
                    last = nc.vector.tensor_tensor(
                        t, t, m_view(first(y) * MW + at(y, y), (1, F - y), (MW, n)), ALU.add)
                    for u, v in parts(0, A) if y >= A else []:
                        t = t_view(y, u, v, ROW[y], n)
                        last = nc.vector.tensor_tensor(
                            t, t, m_view(y * MW + at(u, A), (step_i(u), v - u), (1, n)), ALU.add)
                last.then_inc(tc_step, 1)

            def tile(n, s, begin):
                t = 2 * n + s

                def layout(c):
                    u, v = CHUNKS[c]
                    dve.wait_ge(gathered[s][c], 16 * (v - u) * (n + 1))
                    nc.vector.transpose(XT[s][:, u:v].rearrange("p f i -> p (f i)"),
                                        E[:, s, u:v].rearrange("p f k -> p (f k)")).then_inc(xt_ready, 1)
                    dve.wait_ge(xt_ready, len(CHUNKS) * t + c + 1)
                    if c == 0 and not begin:
                        dve.wait_ge(c2_done, QUADS * (t - 1))
                    for q in range(Q):
                        r = slice(K * q, K * q + K)
                        last = nc.vector.tensor_copy(BD[s][r, :, q, u:v], XT[s][r, u:v].rearrange("p f i -> p i f"))
                    return last

                def products(u, v):
                    for y in range(u, v):
                        r = ROW[y] + (G1_ROWS if group(y) == 2 else 0)
                        w = y - first(y) + 1
                        last = nc.vector.tensor_tensor(
                            P[s][:, :, r:r + w], x_if[:, :, first(y):y + 1],
                            XT[s][:, y, :].unsqueeze(2).broadcast_to([128, NB, w]), ALU.mult)
                    return last

                x_if = XT[s].rearrange("p f i -> p i f")
                layout(0)
                nc.vector.tensor_copy(P[s][:, :, G1_PAIRS:G1_ROWS], x_if[:, :, 0:A])
                products(0, A)
                for c in range(1, len(CHUNKS) - 1):
                    layout(c)
                layout(len(CHUNKS) - 1).then_inc(bd_ready, 1)
                products(A, F).then_inc(p_ready, 1)
                nc.vector.tensor_copy(ids_now[:, s, :],
                                      ids_all[:, bass.ds(t + 2, 1), :].rearrange("p o f -> p (o f)")
                                      ).then_inc(ids_staged, 1)

            tile(0, 0, True)
            fold()
            dve.wait_ge(tc_step, 2)
            nc.vector.memset(P[1][:, :, PCOLS - 1:PCOLS], 1.0).then_inc(zeroed, 1)
            tile(0, 1, True)
            with dve.Fori(1, NPAIR) as n:
                for s in range(2):
                    tile(n, s, False)

        @block.scalar
        def _(act):
            def empty(lo, hi):
                for i in range(lo, hi):
                    kind, g = prep[i]
                    src = prep_bank(i)
                    act.wait_ge(pre_psum, i + 1)
                    if kind == "cols":
                        last = nc.scalar.copy(cols[:], src[:, 0:10])
                    elif kind == "w2t":
                        last = nc.scalar.copy(W2T[:, g[0]:g[-1] + 1, :],
                                              src[:, 0:len(g) * H].rearrange("p (l h) -> p l h", h=H))
                    elif kind == "m":
                        last = nc.scalar.copy(M[:, g[0], :], src[:, 0:MW])
                    elif kind == "dense":
                        for x, t in enumerate(g):
                            last = nc.scalar.copy(
                                densT[:, t * TILE:(t + 1) * TILE].rearrange("p (i q) -> p q i", q=Q),
                                src[0:DC, x * TILE:(x + 1) * TILE].rearrange("p (q i) -> p q i", q=Q))
                    else:
                        last = nc.scalar.copy(TW[:, g[0]:g[-1] + 1, :],
                                              src[:, 0:len(g) * H].rearrange("p (s h) -> p s h", h=H))
                    last.then_inc(pre_out, 1)

            def tile(t):
                for j in range(QUADS):
                    act.wait_ge(c1_done, QUADS * t + j + 1)
                    nc.scalar.copy(CS[0:G1_ROWS, C1_AT:CSLOTS, Q * QUAD * j:Q * QUAD * (j + 1)].rearrange("p l b -> p b l"),
                                   c_bank(pC1, j)[0:G1_ROWS, 0:QUAD * Q * L1].rearrange("p (b l) -> p b l", l=L1)
                                   ).then_inc(c1_out, 1)
                for j in range(QUADS):
                    act.wait_ge(c2_done, QUADS * t + j + 1)
                    nc.scalar.copy(CS[0:G2_ROWS, 0:L2, Q * QUAD * j:Q * QUAD * (j + 1)].rearrange("p l b -> p b l"),
                                   c_bank(pC2, j)[0:G2_ROWS, 0:QUAD * Q * L2].rearrange("p (b l) -> p b l", l=L2)
                                   ).then_inc(c2_out, 1)

            def z_rows(t):
                for d in range(2):
                    act.wait_ge(z_psum, 2 * t + d + 1)
                    nc.scalar.activation(ZT[:, d, :], Z[d], ACT.Identity, bias=kb[:, d:d + 1]).then_inc(z_out, 1)

            def mlp1(t):
                for d in range(N1 // 128):
                    if d % 2 == 0:
                        act.wait_ge(h1_psum, 2 * t + d // 2 + 1)
                    o = nc.scalar.activation(H1T[:, d, :], H1[d][:, TILE * (d % 2):TILE * (d % 2 + 1)], ACT.Relu,
                                             bias=cols[:, d:d + 1])
                    if d % 2 == 1:
                        o.then_inc(h1_out, 1)

            def mlp2(t):
                for d in range(N2 // 128):
                    act.wait_ge(h2_psum, 2 * t + d + 1)
                    nc.scalar.activation(H2T[:, d, :], H2[d], ACT.Relu, bias=cols[:, 4 + d:5 + d]).then_inc(h2_out, 1)

            def mlp3(t):
                act.wait_ge(y_psum, t + 1)
                nc.scalar.copy(Y[:, bass.ds(t * TILE, TILE)].rearrange("p (q i) -> p i q", q=Q),
                               Y_ROW.rearrange("p (i q) -> p i q", q=Q)).then_inc(y_out, 1)

            def z_and_mlp(t):
                z_rows(t)
                mlp1(t)
                mlp2(t)

            empty(0, N_PREP1)
            tile(0)
            empty(N_PREP1, N_PREP)
            z_and_mlp(0)
            tile(1)
            mlp3(0)
            z_and_mlp(1)
            with act.Fori(1, NPAIR) as n:
                for s in range(2):
                    tile(2 * n + s)
                    mlp3(2 * n + s - 1)
                    z_and_mlp(2 * n + s)
            mlp3(NT - 1)

        @block.tensor
        def _(pe):
            def fill(lo, hi):
                for i in range(lo, hi):
                    kind, g = prep[i]
                    dst = prep_bank(i)
                    back = i - (len(BANKS1) if i < N_PREP1 else len(BANKS2))
                    if back >= 0:
                        pe.wait_ge(pre_out, back + 1)
                    if kind == "cols":
                        pe.wait_ge(rows_loaded, 16 * 5)
                        last = nc.tensor.transpose(dst[:, 0:10], rows[:], ident[0:10, 0:10])
                    elif kind == "w2t":
                        pe.wait_ge(w2_loaded, 16)
                        for x, l in enumerate(g):
                            last = nc.tensor.transpose(dst[:, x * H:(x + 1) * H], W2nat[:, :, l], ident[:])
                    elif kind == "m":
                        if g[0] == 0:
                            pe.wait_ge(w1_step, 5)
                            pe.wait_ge(pre_out, W2T_OUT)
                        last = nc.tensor.matmul(dst[:, 0:MW], W2T[:, g[0], :], W1s[:], start=True, stop=True)
                    elif kind == "dense":
                        pe.wait_ge(dense_loaded, 16)
                        for x, t in enumerate(g):
                            last = nc.tensor.transpose(dst[0:DC, x * TILE:(x + 1) * TILE], densN[:, t, :], ident[:])
                    else:
                        pe.wait_ge(tc_step, 2)
                        for x, s in enumerate(g):
                            last = nc.tensor.transpose(dst[:, x * H:(x + 1) * H], Tc[:, s, :], ident[:])
                    last.then_inc(pre_psum, 1)

            def tile(n, s, begin):
                t = 2 * n + s
                pe.wait_ge(bd_ready, t + 1)
                for i in range(NB):
                    j = i // QUAD
                    if i % QUAD == 0 and not (begin and s == 0 and j < len(pC1)):
                        pe.wait_ge(c1_out, QUADS * t + j + 1 - before(pC1, j))
                    at1 = Q * L1 * (i % QUAD)
                    mm = nc.tensor.matmul(c_bank(pC1, j)[0:G1_ROWS, at1:at1 + Q * L1].rearrange("p (q l) -> p q l", l=L1),
                                          P[s][:, i, 0:G1_ROWS], BD[s][:, i, :, T:L2], start=True, stop=True)
                    if i % QUAD == QUAD - 1:
                        mm.then_inc(c1_done, 1)
                pe.wait_ge(p_ready, t + 1)
                for i in range(NB):
                    j = i // QUAD
                    if i % QUAD == 0 and not (begin and s == 0 and j < len(pC2)):
                        pe.wait_ge(c2_out, QUADS * t + j + 1 - before(pC2, j))
                    at2 = Q * L2 * (i % QUAD)
                    mm = nc.tensor.matmul(c_bank(pC2, j)[0:G2_ROWS, at2:at2 + Q * L2].rearrange("p (q l) -> p q l", l=L2),
                                          P[s][:, i, G1_ROWS:PCOLS], BD[s][:, i, :, :], start=True, stop=True)
                    if i % QUAD == QUAD - 1:
                        mm.then_inc(c2_done, 1)

            def z_mm(d, slot, moving, **flags):
                return nc.tensor.matmul(Z[d], TW[0:moving.shape[0], slot, :], moving, **flags)

            def mm1(c, w, moving, **flags):
                return nc.tensor.matmul(H1[c][:, TILE * (c % 2):TILE * (c % 2 + 1)],
                                        w[:, 128 * c:128 * (c + 1)], moving, skip_group_check=True, **flags)

            def z_and_mlp1(t):
                pe.wait_ge(c1_out, QUADS * (t + 1))
                for c in range(N1 // 128):
                    mm1(c, A1d, densT[:, bass.ds(t * TILE, TILE)], start=(c % 2 == 0), stop=False)
                pe.wait_ge(c2_out, QUADS * (t + 1))
                for l in range(F):
                    z_mm(1, l, CS[0:G2_ROWS, l, :], start=(l == 0), stop=False)
                z_mm(0, ONES2, CS[0:G2_PAIRS, ONES2, :], start=True, stop=False)
                pe.wait_ge(g_back, G_BACK * (t + 1))
                for c, r in enumerate(CROSS_ROWS):
                    last = z_mm(0, S_CROSS + c, GX[0:r, c, :], start=False, stop=(c == len(CROSS_ROWS) - 1))
                last.then_inc(z_psum, 1)
                for c in range(PACKS):
                    r = min(128, N_PACK - 128 * c)
                    last = z_mm(1, S_PACK + c, GP[0:r, c, :], start=False, stop=(c == PACKS - 1))
                last.then_inc(z_psum, 1)

                for c0 in range(0, N1 // 128, 2):
                    for d in range(2):
                        if c0 == 0:
                            pe.wait_ge(z_out, 2 * t + d + 1)
                        for c in (c0, c0 + 1):
                            last = mm1(c, A1[:, d, :], ZT[:, d, :], start=False, stop=(d == 1))
                    last.then_inc(h1_psum, 1)

            def mlp2(t, next_tile=None):
                if next_tile is not None:
                    pe.wait_ge(xt_ready, len(CHUNKS) * next_tile + len(CHUNKS) - 1)
                for c0 in range(0, N1 // 128, 2):
                    pe.wait_ge(h1_out, 2 * t + c0 // 2 + 1)
                    for d in range(N2 // 128):
                        for c in (c0, c0 + 1):
                            last = nc.tensor.matmul(H2[d], A2[:, c, 128 * d:128 * (d + 1)], H1T[:, c, :],
                                                    start=(c == 0), stop=(c == N1 // 128 - 1))
                        if c0 + 2 == N1 // 128:
                            last.then_inc(h2_psum, 1)

            def mlp3(t):
                for d in range(N2 // 128):
                    pe.wait_ge(h2_out, 2 * t + d + 1)
                    last = nc.tensor.matmul(Y_ROW, cols[:, 6 + d:7 + d], H2T[:, d, :],
                                            start=(d == 0), stop=(d == N2 // 128 - 1))
                last.then_inc(y_psum, 1)

            pe.wait_ge(ident_ready, 1)
            fill(0, N_PREP1)
            pe.wait_ge(pre_out, N_PREP1)
            tile(0, 0, True)
            fill(N_PREP1, N_PREP)
            pe.wait_ge(pre_out, N_PREP)
            pe.wait_ge(top_loaded, 16 * 3)
            z_and_mlp1(0)
            mlp2(0)
            tile(0, 1, True)
            mlp3(0)
            z_and_mlp1(1)
            with pe.Fori(1, NPAIR) as n:
                for s in range(2):
                    t = 2 * n + s
                    mlp2(t - 1, t)
                    tile(n, s, False)
                    mlp3(t - 1)
                    z_and_mlp1(t)
            mlp2(NT - 1)
            mlp3(NT - 1)


_TABLES = [f"tbl_{f}" for f in range(26)]
_OTHERS = ["dense_ctx", "ids", "W_top1", "b_top1", "W_top2", "b_top2", "W_top3",
           "L0_rec_W1", "L0_rec_b1", "L0_rec_W2", "L0_rec_b2"]


def kernel(**inputs):
    import numpy as _np
    import concourse.bacc as _bacc
    from concourse import mybir as _mybir
    from concourse.bass_utils import run_bass_kernel_spmd as _run

    nc = _bacc.Bacc("TRN2", target_bir_lowering=False, num_devices=1)
    arrays, aps = {}, {}
    for name in _TABLES + _OTHERS:
        a = _np.ascontiguousarray(inputs[name])
        arrays[f"in_{name}"] = a
        aps[name] = nc.dram_tensor(f"in_{name}", a.shape, _mybir.dt.from_np(a.dtype), kind="ExternalInput").ap()
    y = nc.dram_tensor("out_y", (1024, 1), _mybir.dt.float32, kind="ExternalOutput").ap()
    o = {n: aps[n] for n in _OTHERS}
    tower_kernel(nc, o["dense_ctx"], o["ids"], [aps[t] for t in _TABLES], o["W_top1"], o["b_top1"], o["W_top2"],
                 o["b_top2"], o["W_top3"], o["L0_rec_W1"], o["L0_rec_b1"], o["L0_rec_W2"], o["L0_rec_b2"], y)
    r = _run(nc, [arrays], core_ids=[0])
    return r.results[0]["out_y"]
```
